# Optimizing a Trainium2 kernel written in Bass

```python
import numpy as np
import jax
import jax.numpy as jnp

def _softmax(x, axis=-1):
    return jax.nn.softmax(x, axis=axis)

def _gelu(x):
    return jax.nn.gelu(x, approximate=True)

def _silu(x):
    return jax.nn.silu(x)

def _sigmoid(x):
    return jax.nn.sigmoid(x)

def _layernorm(x, axis=-1, eps=1e-05):
    m = jnp.mean(x, axis=axis, keepdims=True)
    v = jnp.var(x, axis=axis, keepdims=True)
    return (x - m) / jnp.sqrt(v + eps)

def _scatter_add(tgt, idx, src, axis=0):
    return tgt.at[idx].add(src)

def _segment_sum(src, seg, n):
    return jax.ops.segment_sum(src, seg, n)
kernel_name = 'mk_dlrm_tower_d1_rec_r8_d95882'

def setup_inputs(seed: int=0):
    np.random.seed(seed)
    _w = jnp.asarray

    def _rec_inputs():
        import jax
        import jax.numpy as jnp
        _tk = jax.random.key(seed)
        ids = jnp.stack([jax.random.randint(jax.random.fold_in(_tk, 200 + f), (2048,), 0, v, jnp.int32) for f, v in enumerate([1000, 12500, 1000, 1000, 125000, 1000, 1250, 1250, 1000, 1250, 1000, 12500, 1000, 12500, 1000, 1250, 1250, 1000, 1000, 12500, 1250, 1250, 1250, 12500, 1000, 1250, 1000])], axis=1)
        tbl_0 = 0.05 * jax.random.normal(jax.random.fold_in(_tk, 500 + 0), (1000, 128), jnp.float32)
        tbl_1 = 0.05 * jax.random.normal(jax.random.fold_in(_tk, 500 + 1), (12500, 128), jnp.float32)
        tbl_2 = 0.05 * jax.random.normal(jax.random.fold_in(_tk, 500 + 2), (1000, 128), jnp.float32)
        tbl_3 = 0.05 * jax.random.normal(jax.random.fold_in(_tk, 500 + 3), (1000, 128), jnp.float32)
        tbl_4 = 0.05 * jax.random.normal(jax.random.fold_in(_tk, 500 + 4), (125000, 128), jnp.float32)
        tbl_5 = 0.05 * jax.random.normal(jax.random.fold_in(_tk, 500 + 5), (1000, 128), jnp.float32)
        tbl_6 = 0.05 * jax.random.normal(jax.random.fold_in(_tk, 500 + 6), (1250, 128), jnp.float32)
        tbl_7 = 0.05 * jax.random.normal(jax.random.fold_in(_tk, 500 + 7), (1250, 128), jnp.float32)
        tbl_8 = 0.05 * jax.random.normal(jax.random.fold_in(_tk, 500 + 8), (1000, 128), jnp.float32)
        tbl_9 = 0.05 * jax.random.normal(jax.random.fold_in(_tk, 500 + 9), (1250, 128), jnp.float32)
        tbl_10 = 0.05 * jax.random.normal(jax.random.fold_in(_tk, 500 + 10), (1000, 128), jnp.float32)
        tbl_11 = 0.05 * jax.random.normal(jax.random.fold_in(_tk, 500 + 11), (12500, 128), jnp.float32)
        tbl_12 = 0.05 * jax.random.normal(jax.random.fold_in(_tk, 500 + 12), (1000, 128), jnp.float32)
        tbl_13 = 0.05 * jax.random.normal(jax.random.fold_in(_tk, 500 + 13), (12500, 128), jnp.float32)
        tbl_14 = 0.05 * jax.random.normal(jax.random.fold_in(_tk, 500 + 14), (1000, 128), jnp.float32)
        tbl_15 = 0.05 * jax.random.normal(jax.random.fold_in(_tk, 500 + 15), (1250, 128), jnp.float32)
        tbl_16 = 0.05 * jax.random.normal(jax.random.fold_in(_tk, 500 + 16), (1250, 128), jnp.float32)
        tbl_17 = 0.05 * jax.random.normal(jax.random.fold_in(_tk, 500 + 17), (1000, 128), jnp.float32)
        tbl_18 = 0.05 * jax.random.normal(jax.random.fold_in(_tk, 500 + 18), (1000, 128), jnp.float32)
        tbl_19 = 0.05 * jax.random.normal(jax.random.fold_in(_tk, 500 + 19), (12500, 128), jnp.float32)
        tbl_20 = 0.05 * jax.random.normal(jax.random.fold_in(_tk, 500 + 20), (1250, 128), jnp.float32)
        tbl_21 = 0.05 * jax.random.normal(jax.random.fold_in(_tk, 500 + 21), (1250, 128), jnp.float32)
        tbl_22 = 0.05 * jax.random.normal(jax.random.fold_in(_tk, 500 + 22), (1250, 128), jnp.float32)
        tbl_23 = 0.05 * jax.random.normal(jax.random.fold_in(_tk, 500 + 23), (12500, 128), jnp.float32)
        tbl_24 = 0.05 * jax.random.normal(jax.random.fold_in(_tk, 500 + 24), (1000, 128), jnp.float32)
        tbl_25 = 0.05 * jax.random.normal(jax.random.fold_in(_tk, 500 + 25), (1250, 128), jnp.float32)
        tbl_26 = 0.05 * jax.random.normal(jax.random.fold_in(_tk, 500 + 26), (1000, 128), jnp.float32)
        _rk = jax.random.fold_in(_tk, 7)
        r_bottom_mlp_out = 4.13588e-05 + 0.999923 * jax.random.normal(jax.random.fold_in(_rk, 101), (2048, 128), jnp.float32)
        W_top1 = 0.0405887 * jax.random.normal(jax.random.fold_in(_tk, 801), (607, 512), jnp.float32)
        W_top2 = 0.0441942 * jax.random.normal(jax.random.fold_in(_tk, 802), (512, 256), jnp.float32)
        W_top3 = 0.0625 * jax.random.normal(jax.random.fold_in(_tk, 803), (256, 1), jnp.float32)
        b_top1 = jnp.zeros((512,), jnp.float32)
        b_top2 = jnp.zeros((256,), jnp.float32)
        return (r_bottom_mlp_out, ids, tbl_0, tbl_1, tbl_2, tbl_3, tbl_4, tbl_5, tbl_6, tbl_7, tbl_8, tbl_9, tbl_10, tbl_11, tbl_12, tbl_13, tbl_14, tbl_15, tbl_16, tbl_17, tbl_18, tbl_19, tbl_20, tbl_21, tbl_22, tbl_23, tbl_24, tbl_25, tbl_26, W_top1, b_top1, W_top2, b_top2, W_top3)
    r_bottom_mlp_out, ids, tbl_0, tbl_1, tbl_2, tbl_3, tbl_4, tbl_5, tbl_6, tbl_7, tbl_8, tbl_9, tbl_10, tbl_11, tbl_12, tbl_13, tbl_14, tbl_15, tbl_16, tbl_17, tbl_18, tbl_19, tbl_20, tbl_21, tbl_22, tbl_23, tbl_24, tbl_25, tbl_26, W_top1, b_top1, W_top2, b_top2, W_top3 = _rec_inputs()

    def _L0_rec_setup():
        import jax, jax.numpy as jnp
        import numpy as np
        NUM_FEATURES = 27

        def _tril_indices(F):
            idx = []
            for i in range(F):
                for j in range(i):
                    idx.append(i * F + j)
            return np.asarray(idx, dtype=np.int32)
        TRIL_IDX = _tril_indices(NUM_FEATURES)
        key = jax.random.key(seed)
        k1, k2 = jax.random.split(key)
        B, F, D = (8192, NUM_FEATURES, 128)
        features = jax.random.normal(k1, (B, F, D), dtype=jnp.float32)
        bottom_mlp_out = jax.random.normal(k2, (B, D), dtype=jnp.float32)
        return {'features': features, 'bottom_mlp_out': bottom_mlp_out}
    _L0_rec_all = _L0_rec_setup()
    _L0_rec_in = {k: v for k, v in _L0_rec_all.items() if k in ()}
    del _L0_rec_all
    return {'r_bottom_mlp_out': r_bottom_mlp_out, 'ids': ids, 'tbl_0': tbl_0, 'tbl_1': tbl_1, 'tbl_2': tbl_2, 'tbl_3': tbl_3, 'tbl_4': tbl_4, 'tbl_5': tbl_5, 'tbl_6': tbl_6, 'tbl_7': tbl_7, 'tbl_8': tbl_8, 'tbl_9': tbl_9, 'tbl_10': tbl_10, 'tbl_11': tbl_11, 'tbl_12': tbl_12, 'tbl_13': tbl_13, 'tbl_14': tbl_14, 'tbl_15': tbl_15, 'tbl_16': tbl_16, 'tbl_17': tbl_17, 'tbl_18': tbl_18, 'tbl_19': tbl_19, 'tbl_20': tbl_20, 'tbl_21': tbl_21, 'tbl_22': tbl_22, 'tbl_23': tbl_23, 'tbl_24': tbl_24, 'tbl_25': tbl_25, 'tbl_26': tbl_26, 'W_top1': W_top1, 'b_top1': b_top1, 'W_top2': W_top2, 'b_top2': b_top2, 'W_top3': W_top3}

def reference(r_bottom_mlp_out, ids, tbl_0, tbl_1, tbl_2, tbl_3, tbl_4, tbl_5, tbl_6, tbl_7, tbl_8, tbl_9, tbl_10, tbl_11, tbl_12, tbl_13, tbl_14, tbl_15, tbl_16, tbl_17, tbl_18, tbl_19, tbl_20, tbl_21, tbl_22, tbl_23, tbl_24, tbl_25, tbl_26, W_top1, b_top1, W_top2, b_top2, W_top3):
    import jax
    import jax.numpy as jnp

    def _L0_rec_ref(features, bottom_mlp_out):
        import jax, jax.numpy as jnp
        import numpy as np
        NUM_FEATURES = 27

        def _tril_indices(F):
            idx = []
            for i in range(F):
                for j in range(i):
                    idx.append(i * F + j)
            return np.asarray(idx, dtype=np.int32)
        TRIL_IDX = _tril_indices(NUM_FEATURES)
        B = features.shape[0]
        F = features.shape[1]
        interactions = jnp.einsum('bfd,bgd->bfg', features, features)
        interactions = interactions.reshape(B, F * F)
        x = interactions[:, TRIL_IDX]
        return jnp.concatenate([bottom_mlp_out, x], axis=1)
    e = jnp.stack([tbl_0[ids[:, 0]], tbl_1[ids[:, 1]], tbl_2[ids[:, 2]], tbl_3[ids[:, 3]], tbl_4[ids[:, 4]], tbl_5[ids[:, 5]], tbl_6[ids[:, 6]], tbl_7[ids[:, 7]], tbl_8[ids[:, 8]], tbl_9[ids[:, 9]], tbl_10[ids[:, 10]], tbl_11[ids[:, 11]], tbl_12[ids[:, 12]], tbl_13[ids[:, 13]], tbl_14[ids[:, 14]], tbl_15[ids[:, 15]], tbl_16[ids[:, 16]], tbl_17[ids[:, 17]], tbl_18[ids[:, 18]], tbl_19[ids[:, 19]], tbl_20[ids[:, 20]], tbl_21[ids[:, 21]], tbl_22[ids[:, 22]], tbl_23[ids[:, 23]], tbl_24[ids[:, 24]], tbl_25[ids[:, 25]], tbl_26[ids[:, 26]]], axis=1)
    z = _L0_rec_ref(e, r_bottom_mlp_out)
    z = z.reshape(z.shape[0], -1)
    h = jnp.concatenate([z, r_bottom_mlp_out], axis=1)
    h = jnp.maximum(h @ W_top1 + b_top1, 0.0)
    h = jnp.maximum(h @ W_top2 + b_top2, 0.0)
    y = h @ W_top3
    return y

_drawn_inputs = setup_inputs


def setup_inputs(seed=0):
    import zlib

    import numpy as np

    out = dict(_drawn_inputs(seed))
    spreads = {'b_top1': (0.0, 0.1), 'b_top2': (0.0, 0.1)}
    factors = {'tbl_0': 4.829,
     'tbl_1': 5.058,
     'tbl_2': 4.546,
     'tbl_3': 4.12,
     'tbl_4': 4.782,
     'tbl_5': 4.461,
     'tbl_6': 4.805,
     'tbl_7': 4.137,
     'tbl_8': 4.611,
     'tbl_9': 4.958,
     'tbl_10': 4.334,
     'tbl_11': 4.484,
     'tbl_12': 4.469,
     'tbl_13': 4.413,
     'tbl_14': 4.791,
     'tbl_15': 4.822,
     'tbl_16': 4.761,
     'tbl_17': 4.917,
     'tbl_18': 4.198,
     'tbl_19': 4.321,
     'tbl_20': 4.365,
     'tbl_21': 4.975,
     'tbl_22': 4.643,
     'tbl_23': 5.008,
     'tbl_24': 4.443,
     'tbl_25': 4.963,
     'tbl_26': 4.415}
    for name, (base, spread) in spreads.items():
        noise = np.random.default_rng([zlib.crc32(name.encode()), seed]).standard_normal(out[name].shape)
        drawn = base * np.exp(spread * noise) if base else spread * noise
        out[name] = jnp.asarray(drawn.astype(out[name].dtype))
    for name, factor in factors.items():
        out[name] = (out[name] * factor).astype(out[name].dtype)
    return out
```

```python
import concourse.bass as bass
from concourse import mybir
from contextlib import ExitStack

BATCH, FEATURES, D = 2048, 27, 128
SMALL_VOCAB = 1000
ONEHOT_TABLES = 8
BLOCK, HALF, TILE = 512, 256, 128
BLOCKS, TILES = BATCH // BLOCK, BLOCK // TILE
PAD = 32
GROUP = 4
JG = BLOCK // GROUP
PG = FEATURES - 1
PAIRS = FEATURES * PG // 2
CHUNK = PAIRS // 3
H1, H2 = 512, 256
HIGH, LOW = 0, 1


def slots(vocabs):
    onehot = [f for f in range(FEATURES) if vocabs[f] == SMALL_VOCAB][:ONEHOT_TABLES]
    gathered = [f for f in range(FEATURES) if f not in onehot]
    return gathered, onehot


def pair_rows(order):
    rows = []
    for g in range(PG):
        for f in range(g + 1, FEATURES):
            a, b = max(order[f], order[g]), min(order[f], order[g])
            rows.append(D + a * (a - 1) // 2 + b)
    return rows


def dlrm_tower(nc, bottom, ids, ids_onehot, tables, w_bottom_a, w_pairs, w_bottom_b, b1, w2, b2, w3, out):
    fp32, fp32r, i32 = mybir.dt.float32, mybir.dt.float32r, mybir.dt.int32
    ALU = mybir.AluOpType
    ACT = mybir.ActivationFunctionType

    gathered, onehot = slots([t.shape[0] for t in tables])
    NG, NO = len(gathered), len(onehot)
    VB = 8
    VP = SMALL_VOCAB // VB
    VP_A = VP // 16 * 16
    FQ = 4
    TQ = (NG + FQ - 1) // FQ
    RAWS = 5
    OP = NO // 2
    assert NO % 2 == 0 and VP <= 128

    def hot_use(half, p):
        return [("hot", half, p)]

    def tile_use(t):
        return [("tile", t, u) for u in range(TQ)]

    BUILD_ORDER = (hot_use(0, 0) + hot_use(0, 1) + tile_use(0) + hot_use(0, 2) + hot_use(0, 3) + tile_use(1)
                   + hot_use(1, 0) + hot_use(1, 1) + tile_use(2)[0:2] + hot_use(1, 2) + tile_use(2)[2:4]
                   + hot_use(1, 3) + tile_use(2)[4:5] + tile_use(3))
    BUILDS = len(BUILD_ORDER)
    assert OP == 4 and TQ == 5 and BUILDS % 2 == 0

    def nth(*use):
        return BUILD_ORDER.index(use)

    def tile_end(t):
        return nth("tile", t, TQ - 1) + 1

    def hot_end(half, p):
        return nth("hot", half, p) + 1

    HOTS = 2 * 2 * NO
    GB = 8
    GU = TILE // GROUP // GB
    GRAMS = TILES * GU
    GC = GROUP * PG
    RB = 4
    RG = (PG + RB - 1) // RB
    M1, M2 = H1 // 128, H2 // 128
    USE_R, USE_G, USE_X = 0, 1, 1 + RG
    USE_1 = USE_X + 3
    USE_2 = USE_1 + M1
    USE_Y = USE_2 + M2
    DENSE = USE_Y + 1
    reader = ["dve"] + ["dve" if u % 2 == 0 else "act" for u in range(RG)] + ["dve"] * 3 + ["dve"] * M1 + ["act"] * M2 + ["act"]
    HIGHS = 1 + 3 + M1
    assert DENSE % 2 == 0 and len(reader) == DENSE

    def read_by(engine, upto):
        return reader[:upto].count(engine)

    ctx = ExitStack()
    with ctx:
        def sb(name, shape, dt):
            return ctx.enter_context(nc.sbuf_tensor(name, shape, dt))

        def sem(name):
            return ctx.enter_context(nc.semaphore(name))

        KIB = 1024
        arena_at = (nc.sbuf_base + 31) // 32 * 32
        arena = sb("arena", [128, 20 * KIB // 4], fp32)

        weight_arena_at = (nc.sbuf_base + 31) // 32 * 32
        weight_arena = sb("weight_arena", [128, 12 * KIB // 4], fp32)

        def in_arena(name, shape, dt, at):
            return nc.alloc_sbuf_tensor_at(name, shape, dt, offset=arena_at + at)

        def in_weight_arena(name, shape, dt, at):
            return nc.alloc_sbuf_tensor_at(name, shape, dt, offset=weight_arena_at + at)

        raw = in_arena("raw", [128, RAWS, VB * D], fp32, 0)
        w1p_raw = in_weight_arena("w1p_raw", [CHUNK, 3, H1], fp32, 0)
        w1b_raw = in_weight_arena("w1b_raw", [128, H1], fp32, 6 * KIB)
        w2_raw = in_weight_arena("w2_raw", [128, M1, H2], fp32, 8 * KIB)
        pairT = in_weight_arena("pairT", [CHUNK, 2, 3, BLOCK], fp32r, 0)
        gram = in_arena("gram", [128, PG, JG], fp32, 0)
        h1 = in_arena("h1", [128, 2, M1, BLOCK], fp32r, 0)
        h2 = in_arena("h2", [128, M2, BLOCK], fp32, 16 * KIB)

        embT = sb("embT", [128, HALF, PAD], fp32)
        rows = sb("rows", [128, 2, NG * D], fp32)
        idx = sb("idx", [128, TILES, FEATURES], i32)
        table = sb("table", [128, NO, 2, VB * D], fp32r)
        id_raw = sb("id_raw", [128, 2, 2, HALF], i32)
        hot = sb("hot", [128, 2, 2, VB // 2, HALF], fp32r)
        vocab_i = sb("vocab_i", [128, VB], i32)
        vocab = sb("vocab", [128, VB], fp32)
        ident = sb("ident", [128, 128], fp32)
        packed = sb("packed", [128, GROUP, PAIRS], fp32)
        w1b_more = packed[:, 0:2, 0:H1 // 2]
        bot = sb("bot", [128, GROUP, D], fp32)
        botT = sb("botT", [128, 2, BLOCK], fp32r)
        w1p = sb("w1p", [CHUNK, 2, 3, H1], fp32r)
        w1b = sb("w1b", [128, 2, H1], fp32r)
        w2s = sb("w2s", [128, 2, M1, H2], fp32r)
        w3s = sb("w3s", [128, M2], fp32)
        b1s = sb("b1s", [128, M1], fp32)
        b2s = sb("b2s", [128, M2], fp32)
        y = sb("y", [1, BLOCK], fp32)

        ps_build = [ctx.enter_context(nc.psum_tensor(f"ps_build{i}", [128, 512], fp32)) for i in range(2)]
        ps_gram = [ctx.enter_context(nc.psum_tensor(f"ps_gram{i}", [128, 1024], fp32)) for i in range(2)]
        ps_dense = [ctx.enter_context(nc.psum_tensor(f"ps_dense{i}", [128, 512], fp32)) for i in range(2)]

        consts_made = sem("consts_made")
        weights_in = sem("weights_in")
        idx_in = [sem(f"idx_in{t}") for t in range(TILES)]
        rows_in = [sem(f"rows_in{s}") for s in range(2)]
        raw_in = [sem(f"raw_in{s}") for s in range(RAWS)]
        id_in = [sem(f"id_in{s}") for s in range(2)]
        bot_in = sem("bot_in")
        pad_set = sem("pad_set")
        table_high = sem("table_high")
        table_low = sem("table_low")
        w1b_added = sem("w1b_added")
        weights_high = sem("weights_high")
        weights_low = sem("weights_low")
        loads_begun = sem("loads_begun")
        gathers_begun = sem("gathers_begun")
        hot_made = sem("hot_made")
        hot_used = sem("hot_used")
        built = sem("built")
        emb_done = sem("emb_done")
        grammed = sem("grammed")
        gram_dve = sem("gram_dve")
        gram_act = sem("gram_act")
        densed = sem("densed")
        relu_done = sem("relu_done")
        high_made = sem("high_made")
        dense_dve = sem("dense_dve")
        dense_act = sem("dense_act")
        dve_step = sem("dve_step")
        out_done = sem("out_done")
        dense_read = {"dve": dense_dve, "act": dense_act}
        WEIGHT_LOADS = 7
        TILE_BETWEEN = [(0, 1), (2,), (3, 4), ()]

        def gram_pieces(t, u, k):
            src = ps_gram[u % 2][PAD * k:PAD * (k + 1), :].rearrange("p (h c) -> p h c", h=2)
            src = src[:, :, 0:GB // 2 * GC].rearrange("p h (g c) -> p c h g", g=GB // 2)[:, k * PG:(k + 1) * PG]
            j = (t * GU + u) * GB
            dst = gram[PAD * k:PAD * (k + 1), :, j:j + GB].rearrange("p f (h g) -> p f h g", h=2)
            return dst, src

        def pack_pieces(u):
            for g in range(u * RB, min((u + 1) * RB, PG)):
                n = PG - g
                at = PAIRS - n * (n + 1) // 2
                src = ps_dense[(USE_G + u) % 2][:, (g % RB) * 128:(g % RB + 1) * 128]
                yield packed[:, :, at:at + n], src.rearrange("p (k f) -> p k f", k=GROUP)[:, :, g + 1:FEATURES]

        block = ctx.enter_context(nc.Block())

        @block.sync
        def _(sp):
            def load_idx(at, t):
                sp.dma_start(idx[:, t, :], ids[bass.ds(at, BLOCK), :][t * TILE:(t + 1) * TILE, :]).then_inc(idx_in[t], 16)

            def load_ids(at, n):
                half, p = n // OP, n % OP
                src = ids_onehot[2 * p:2 * p + 2, bass.ds(at, BLOCK)][:, half * HALF:(half + 1) * HALF]
                sp.dma_start(id_raw[:, n % 2, :, :], src.unsqueeze(0).broadcast_to([128, 2, HALF])).then_inc(id_in[n % 2], 16)

            def load_bottom(at):
                src = bottom[bass.ds(at, BLOCK), :].rearrange("(j k) d -> j k d", k=GROUP)
                sp.dma_start(bot[:, :, :], src).then_inc(bot_in, 16)

            def load_table(q):
                src = tables[onehot[q]].rearrange("(p v) d -> p (v d)", v=VB)
                sp.dma_start(raw[0:VP_A, q % RAWS, :], src[0:VP_A, :]).then_inc(raw_in[q % RAWS], 16)
                sp.dma_start(raw[VP_A:VP, q % RAWS, :], src[VP_A:VP, :]).then_inc(raw_in[q % RAWS], 16)

            def store(i, at):
                sp.wait_ge(dense_act, read_by("act", DENSE) * (i + 1))
                sp.sem_inc(loads_begun, 1)
                sp.dma_start(out[bass.ds(at, BLOCK), :].rearrange("b o -> o b"), y[:, :]).then_inc(out_done, 16)

            load_idx(0, 0)
            load_table(0)
            load_ids(0, 0)
            load_table(1)
            load_ids(0, 1)
            load_table(2)
            load_table(3)
            load_idx(0, 1)
            load_table(4)
            load_idx(0, 2)
            load_idx(0, 3)
            for q in range(RAWS, NO):
                sp.wait_ge(table_low, q - RAWS + 1)
                load_table(q)
            load_bottom(0)
            for n in range(2, 2 * OP):
                sp.wait_ge(hot_made, 4 * (n - 1))
                load_ids(0, n)
            with sp.Fori(1, BLOCKS) as i:
                at = sp.snap(i * BLOCK)
                before = sp.snap(i * BLOCK - BLOCK)

                def next_idx(t):
                    sp.wait_ge(rows_in[t % 2], 16 * NG * (2 * i - 1 + t // 2))
                    sp.sem_inc(loads_begun, 1)
                    load_idx(at, t)

                def next_ids(n):
                    sp.wait_ge(hot_made, HOTS * i + 4 * (n - 1))
                    sp.sem_inc(loads_begun, 1)
                    load_ids(at, n)

                next_idx(0)
                next_idx(1)
                next_idx(2)
                next_ids(0)
                next_ids(1)
                next_idx(3)
                sp.wait_ge(densed, DENSE * (i - 1) + USE_R + 1)
                sp.sem_inc(loads_begun, 1)
                load_bottom(at)
                for n in range(2, OP + 1):
                    next_ids(n)
                store(i - 1, before)
                for n in range(OP + 1, 2 * OP):
                    next_ids(n)
            store(BLOCKS - 1, BATCH - BLOCK)
            sp.wait_ge(out_done, 16 * BLOCKS)

        @block.gpsimd
        def _(pool):
            nc.gpsimd.iota(vocab_i[:, :], pattern=[[1, VB]], base=0, channel_multiplier=VB).then_inc(consts_made, 1)
            nc.gpsimd.memset(ident[:, :], 0.0).then_inc(consts_made, 1)
            pool.wait_ge(consts_made, 2)
            nc.gpsimd.affine_select(out=ident[:, :], in_=ident[:, :], compare_op=ALU.not_equal, fill=1.0, base=0,
                                    pattern=[[-1, 128]], channel_multiplier=1).then_inc(consts_made, 1)

            def gather(i, t):
                pool.wait_ge(idx_in[t], 16 * (i + 1))
                if t >= 2:
                    pool.wait_ge(built, BUILDS * i + tile_end(t - 2))
                elif not (isinstance(i, int) and i == 0):
                    pool.wait_ge(built, BUILDS * (i - 1) + tile_end(t + 2))
                pool.sem_inc(gathers_begun, 1)
                for s, f in enumerate(gathered):
                    nc.gpsimd.indirect_dma_start(
                        rows[:, t % 2, s * D:(s + 1) * D], None, tables[f],
                        bass.IndirectOffsetOnAxis(idx[:, t, f:f + 1], 0)).then_inc(rows_in[t % 2], 16)

            for t in range(TILES):
                gather(0, t)
            with pool.Fori(1, BLOCKS) as i:
                for t in range(TILES):
                    gather(i, t)

        @block.vector
        def _(dve):
            def low_part(dst, whole, high):
                return nc.vector.tensor_tensor(dst, whole, high.bitcast(fp32), ALU.subtract)

            def split_table(q):
                dve.wait_ge(table_high, q + 1)
                low_part(table[0:VP, q, LOW, :], raw[0:VP, q % RAWS, :], table[0:VP, q, HIGH, :]).then_inc(table_low, 1)

            def make_hot(i, half, p, parts=range(4)):
                n = half * OP + p
                first = isinstance(i, int) and i == 0
                if 0 in parts:
                    dve.wait_ge(id_in[n % 2], 16 * (OP * i + n // 2 + 1))
                for part in parts:
                    q, v0 = part // 2, part % 2
                    if n > 0 and part < 3:
                        dve.wait_ge(hot_used, 3 * (2 * OP * i + n - 1) + part + 1)
                    elif n > 0:
                        dve.wait_ge(built, BUILDS * i + hot_end((n - 1) // OP, (n - 1) % OP))
                    elif not first and part < 3:
                        dve.wait_ge(hot_used, 3 * (2 * OP * i - 1) + part + 1)
                    elif not first:
                        dve.wait_ge(built, BUILDS * (i - 1) + hot_end(1, OP - 1))
                    for v in range(VB // 2):
                        row = v0 * VB // 2 + v
                        last = nc.vector.tensor_scalar(hot[0:VP, q, v0, v, :], id_raw[0:VP, n % 2, q, :],
                                                       vocab[0:VP, row:row + 1], None, ALU.is_equal)
                    last.then_inc(hot_made, 1)

            def empty_gram(i, t, u):
                dve.wait_ge(grammed, GRAMS * i + t * GU + u + 1)
                for k in (0, 1):
                    last = nc.vector.tensor_copy(*gram_pieces(t, u, k))
                last.then_inc(gram_dve, 1)

            def pairs_of_half(i, half, next_hot):
                for n in range(2 * GU):
                    empty_gram(i, 2 * half + n // GU, n % GU)
                    if next_hot and n % 2:
                        make_hot(*next_hot, [n // 2])

            def dense_low(i, w, high_n, dst, high, rows_used=128):
                dve.wait_ge(high_made, HIGHS * i + high_n + 1)
                low_part(dst, ps_dense[w % 2][0:rows_used, :], high).then_inc(dense_dve, 1)

            def pack(i, u):
                dve.wait_ge(densed, DENSE * i + USE_G + u + 1)
                for dst, src in pack_pieces(u):
                    last = nc.vector.tensor_copy(dst, src)
                last.then_inc(dense_dve, 1)

            def dense(i, hots):
                dense_low(i, USE_R, 0, botT[:, LOW, :], botT[:, HIGH, :])
                for u in range(0, RG, 2):
                    pack(i, u)
                    hots(1, u // 2)
                for c in range(3):
                    dense_low(i, USE_X + c, 1 + c, pairT[:, LOW, c, :], pairT[:, HIGH, c, :], CHUNK)
                hots(2, 0)
                for m in range(M1):
                    if m < 3:
                        hots(2, m + 1)
                    dense_low(i, USE_1 + m, 4 + m, h1[:, LOW, m, :], h1[:, HIGH, m, :])

            def add_w1b():
                dve.wait_ge(weights_in, 16 * WEIGHT_LOADS)
                halves = w1b_raw[:, :].rearrange("p (a b) -> p a b", a=2)
                nc.vector.tensor_tensor(halves, halves, w1b_more, ALU.add).then_inc(w1b_added, 1)

            def split_weights():
                dve.wait_ge(weights_high, 3)
                low_part(w1p[:, LOW, :, :], w1p_raw[:, :, :], w1p[:, HIGH, :, :]).then_inc(weights_low, 1)
                low_part(w1b[:, LOW, :], w1b_raw[:, :], w1b[:, HIGH, :]).then_inc(weights_low, 1)
                low_part(w2s[:, LOW, :, :], w2_raw[:, :, :], w2s[:, HIGH, :, :]).then_inc(weights_low, 1)

            def block_work(i, more):
                make_hot(i, 0, 3)
                pairs_of_half(i, 0, (i, 1, 0))
                for p in range(1, OP):
                    make_hot(i, 1, p)
                if isinstance(i, int) and i == 0:
                    split_weights()
                pairs_of_half(i, 1, (i + 1, 0, 0) if more else None)

            nc.vector.memset(embT[:, :, FEATURES:PAD], 0.0).then_inc(pad_set, 1)
            dve.wait_ge(consts_made, 1)
            nc.vector.tensor_copy(vocab[:, :], vocab_i[:, :]).then_inc(dve_step, 1)
            dve.wait_ge(dve_step, 1)
            for p in range(OP):
                split_table(2 * p)
                split_table(2 * p + 1)
                if p < OP - 1:
                    make_hot(0, 0, p)
            add_w1b()
            block_work(0, True)
            with dve.Fori(1, BLOCKS - 1) as i:
                dense(i - 1, lambda p, part: make_hot(i, 0, p, [part]))
                block_work(i, True)
            dense(BLOCKS - 2, lambda p, part: make_hot(BLOCKS - 1, 0, p, [part]))
            block_work(BLOCKS - 1, False)
            dense(BLOCKS - 1, lambda p, part: None)

        @block.scalar
        def _(act):
            def load_weights():
                for dst, src in ((w1b_raw[:, :], w_bottom_a), (w1b_more, w_bottom_b.rearrange("p (a b) -> p a b", a=2)),
                                 (w1p_raw[:, :, :], w_pairs.rearrange("(c p) h -> p c h", c=3)),
                                 (w2_raw[:, :, :], w2.rearrange("(c p) h -> p c h", p=128)),
                                 (w3s[:, :], w3), (b1s[:, :], b1), (b2s[:, :], b2)):
                    act.dma_start(dst, src).then_inc(weights_in, 16)

            def split_table(q):
                act.wait_ge(raw_in[q % RAWS], 32 * (q // RAWS + 1))
                nc.scalar.copy(table[0:VP, q, HIGH, :], raw[0:VP, q % RAWS, :]).then_inc(table_high, 1)

            def split_weights():
                act.wait_ge(weights_in, 16 * WEIGHT_LOADS)
                nc.scalar.copy(w1p[:, HIGH, :, :], w1p_raw[:, :, :]).then_inc(weights_high, 1)
                nc.scalar.copy(w2s[:, HIGH, :, :], w2_raw[:, :, :]).then_inc(weights_high, 1)
                act.wait_ge(w1b_added, 1)
                nc.scalar.copy(w1b[:, HIGH, :], w1b_raw[:, :]).then_inc(weights_high, 1)

            def emb_hot(i, half, p):
                s = nth("hot", half, p)
                act.wait_ge(built, BUILDS * i + s + 1)
                nc.scalar.copy(embT[:, :, NG + 2 * p:NG + 2 * p + 2],
                               ps_build[s % 2][:, :].rearrange("p (q b) -> p b q", q=2)).then_inc(emb_done, 1)

            def emb_tile(i, t, banks=range(TQ)):
                for u in banks:
                    s = nth("tile", t, u)
                    n = min(FQ, NG - u * FQ)
                    act.wait_ge(built, BUILDS * i + s + 1)
                    src = ps_build[s % 2][:, 0:n * 128].rearrange("p (f b) -> p b f", f=n)
                    b = t % 2 * TILE
                    nc.scalar.copy(embT[:, b:b + TILE, u * FQ:u * FQ + n], src).then_inc(emb_done, 1)

            def empty_gram(i, t, u):
                act.wait_ge(grammed, GRAMS * i + t * GU + u + 1)
                for k in (2, 3):
                    last = nc.scalar.copy(*gram_pieces(t, u, k))
                last.then_inc(gram_act, 1)

            def pairs_of_half(i, half):
                t = 2 * half
                for u in range(GU):
                    empty_gram(i, t, u)
                    emb_tile(i, t + 1, TILE_BETWEEN[u])
                for u in range(GU):
                    empty_gram(i, t + 1, u)

            def dense_high(i, w, dst, rows_used=128):
                act.wait_ge(densed, DENSE * i + w + 1)
                nc.scalar.copy(dst, ps_dense[w % 2][0:rows_used, :]).then_inc(high_made, 1)

            def relayout(i):
                dense_high(i, USE_R, botT[:, HIGH, :])
                for u in range(RG):
                    if reader[USE_G + u] == "act":
                        act.wait_ge(densed, DENSE * i + USE_G + u + 1)
                        for dst, src in pack_pieces(u):
                            last = nc.scalar.copy(dst, src)
                        last.then_inc(dense_act, 1)

            def pair_highs(i):
                for c in range(3):
                    dense_high(i, USE_X + c, pairT[:, HIGH, c, :], CHUNK)

            def layer1(i):
                for m in range(M1):
                    w = USE_1 + m
                    act.wait_ge(densed, DENSE * i + w + 1)
                    nc.scalar.activation(ps_dense[w % 2][:, :], ps_dense[w % 2][:, :], ACT.Relu,
                                         bias=b1s[:, m:m + 1]).then_inc(relu_done, 1)
                    act.wait_ge(relu_done, M1 * i + m + 1)
                    nc.scalar.copy(h1[:, HIGH, m, :], ps_dense[w % 2][:, :]).then_inc(high_made, 1)

            def layer2(i, m):
                w = USE_2 + m
                act.wait_ge(densed, DENSE * i + w + 1)
                nc.scalar.activation(h2[:, m, :], ps_dense[w % 2][:, :], ACT.Relu,
                                     bias=b2s[:, m:m + 1]).then_inc(dense_act, 1)

            def layer3(i):
                act.wait_ge(densed, DENSE * i + USE_Y + 1)
                nc.scalar.copy(y[:, :].rearrange("p (j k) -> p k j", k=GROUP),
                               ps_dense[USE_Y % 2][0:1, :].rearrange("p (k j) -> p k j", k=GROUP)).then_inc(dense_act, 1)

            def second_half(i):
                emb_hot(i, 1, 0)
                emb_hot(i, 1, 1)
                emb_tile(i, 2, [0, 1])
                if isinstance(i, int):
                    split_weights()
                emb_hot(i, 1, 2)
                emb_tile(i, 2, [2, 3])
                emb_hot(i, 1, 3)
                emb_tile(i, 2, [4])
                pairs_of_half(i, 1)

            for q in range(NO):
                split_table(q)
                if q == 1:
                    load_weights()
                if q == 3:
                    emb_hot(0, 0, 0)
                if q == 5:
                    emb_hot(0, 0, 1)
            emb_tile(0, 0)
            emb_hot(0, 0, 2)
            emb_hot(0, 0, 3)
            pairs_of_half(0, 0)
            second_half(0)
            with act.Fori(1, BLOCKS) as i:
                relayout(i - 1)
                emb_hot(i, 0, 0)
                pair_highs(i - 1)
                emb_hot(i, 0, 1)
                layer1(i - 1)
                emb_tile(i, 0)
                layer2(i - 1, 0)
                layer2(i - 1, 1)
                emb_hot(i, 0, 2)
                emb_hot(i, 0, 3)
                layer3(i - 1)
                pairs_of_half(i, 0)
                second_half(i)
                act.wait_ge(out_done, 16 * i)
            relayout(BLOCKS - 1)
            pair_highs(BLOCKS - 1)
            layer1(BLOCKS - 1)
            layer2(BLOCKS - 1, 0)
            layer2(BLOCKS - 1, 1)
            layer3(BLOCKS - 1)

        @block.tensor
        def _(pe):
            def build_bank(i, s):
                if s >= 2:
                    pe.wait_ge(emb_done, BUILDS * i + s - 1)
                elif not (isinstance(i, int) and i == 0):
                    pe.wait_ge(emb_done, BUILDS * i)
                return ps_build[s % 2]

            def dense_bank(i, w):
                if w >= 2:
                    e = reader[w - 2]
                    pe.wait_ge(dense_read[e], read_by(e, DENSE) * i + read_by(e, w - 1))
                return ps_dense[w % 2]

            def onehot_pair(i, half, p, parts=range(4)):
                n = half * OP + p
                s = nth("hot", half, p)
                bank = build_bank(i, s) if 0 in parts else ps_build[s % 2]
                for part in parts:
                    q, v0 = part // 2, part % 2
                    if isinstance(i, int) and i == 0 and half == 0 and v0 == 0:
                        pe.wait_ge(table_low, 2 * p + q + 1)
                    pe.wait_ge(hot_made, HOTS * i + 4 * n + part + 1)
                    for v in range(VB // 2):
                        row = (v0 * VB // 2 + v) * D
                        for bits in (HIGH, LOW):
                            last = nc.tensor.matmul(bank[:, q * HALF:(q + 1) * HALF],
                                                    table[0:VP, 2 * p + q, bits, row:row + D],
                                                    hot[0:VP, q, v0, v, :], start=(v0 == v == bits == 0),
                                                    stop=(v0 == 1 and v == VB // 2 - 1 and bits == LOW))
                    last.then_inc(hot_used if part < 3 else built, 1)

            def transpose_tile(i, t, banks=range(TQ)):
                if 0 in banks:
                    pe.wait_ge(rows_in[t % 2], 16 * NG * (2 * i + t // 2 + 1))
                for u in banks:
                    bank = build_bank(i, nth("tile", t, u))
                    for f in range(min(FQ, NG - u * FQ)):
                        last = nc.tensor.transpose(bank[:, f * 128:(f + 1) * 128],
                                                   rows[:, t % 2, (u * FQ + f) * D:(u * FQ + f + 1) * D], ident[:, :])
                    last.then_inc(built, 1)

            def pair_products(i, t, buffers=range(GU)):
                if 0 in buffers:
                    pe.wait_ge(emb_done, BUILDS * i + max(tile_end(t), hot_end(t // 2, OP - 1)))
                for u in buffers:
                    v = t * GU + u
                    if v >= 2:
                        pe.wait_ge(gram_dve, GRAMS * i + v - 1)
                        pe.wait_ge(gram_act, GRAMS * i + v - 1)
                    for g in range(GB):
                        at = t % 2 * TILE + (u * GB + g) * GROUP
                        c = g // (GB // 2) * 512 + g % (GB // 2) * GC
                        last = nc.tensor.matmul(ps_gram[u % 2][:, c:c + GC],
                                                embT[:, at:at + GROUP, :].rearrange("p k f -> p (k f)"),
                                                embT[:, at:at + GROUP, 0:PG], start=True, stop=True)
                    last.then_inc(grammed, 1)

            def bottom_back(i):
                pe.wait_ge(bot_in, 16 * (i + 1))
                bank = dense_bank(i, USE_R)
                for k in range(GROUP):
                    last = nc.tensor.transpose(bank[:, k * JG:(k + 1) * JG], bot[:, k, :], ident[:, :])
                last.then_inc(densed, 1)

            def relayout(i, banks):
                if 0 in banks:
                    pe.wait_ge(gram_dve, GRAMS * (i + 1))
                    pe.wait_ge(gram_act, GRAMS * (i + 1))
                for u in banks:
                    bank = dense_bank(i, USE_G + u)
                    for g in range(u * RB, min((u + 1) * RB, PG)):
                        last = nc.tensor.transpose(bank[:, (g % RB) * 128:(g % RB + 1) * 128], gram[:, g, :], ident[:, :])
                    last.then_inc(densed, 1)

            def wait_dense(i, upto):
                for e in ("dve", "act"):
                    pe.wait_ge(dense_read[e], read_by(e, DENSE) * i + read_by(e, upto))

            def pairs_back(i, chunks):
                if 0 in chunks:
                    wait_dense(i, USE_X)
                for c in chunks:
                    bank = dense_bank(i, USE_X + c)
                    for k in range(GROUP):
                        last = nc.tensor.transpose(bank[0:CHUNK, k * JG:(k + 1) * JG],
                                                   packed[:, k, c * CHUNK:(c + 1) * CHUNK], ident[:, :])
                    last.then_inc(densed, 1)

            def split_product(bank, w, x, first=False, end=False):
                for m, (a, b) in enumerate(((HIGH, HIGH), (HIGH, LOW), (LOW, HIGH))):
                    last = nc.tensor.matmul(bank[:, :], w(a), x(b), start=(first and m == 0), stop=(end and m == 2))
                return last

            def layer1(i):
                for m in range(M1):
                    bank = dense_bank(i, USE_1 + m)
                    cols = slice(m * 128, (m + 1) * 128)
                    if m == 0:
                        wait_dense(i, USE_G)
                    split_product(bank, lambda a: w1b[:, a, cols], lambda b: botT[:, b, :], first=True)
                    if m == 0:
                        wait_dense(i, USE_1)
                    for c in range(3):
                        last = split_product(bank, lambda a: w1p[:, a, c, cols], lambda b: pairT[:, b, c, :], end=(c == 2))
                    last.then_inc(densed, 1)

            def layer2(i, m, chunks=range(M1)):
                w = USE_2 + m
                if m == 0 and 0 in chunks:
                    wait_dense(i, USE_2)
                bank = dense_bank(i, w) if 0 in chunks else ps_dense[w % 2]
                cols = slice(m * 128, (m + 1) * 128)
                for c in chunks:
                    last = split_product(bank, lambda a: w2s[:, a, c, cols], lambda b: h1[:, b, c, :],
                                         first=(c == 0), end=(c == M1 - 1))
                if M1 - 1 in chunks:
                    last.then_inc(densed, 1)

            def layer3(i):
                wait_dense(i, USE_Y)
                bank = dense_bank(i, USE_Y)
                for c in range(M2):
                    last = nc.tensor.matmul(bank[0:1, :], w3s[:, c:c + 1], h2[:, c, :], start=(c == 0), stop=(c == M2 - 1))
                last.then_inc(densed, 1)

            def pairs_of_half(i, half):
                t = 2 * half
                for u in range(GU):
                    pair_products(i, t, [u])
                    transpose_tile(i, t + 1, TILE_BETWEEN[u])
                pair_products(i, t + 1)

            def second_half(i):
                onehot_pair(i, 1, 0)
                onehot_pair(i, 1, 1)
                transpose_tile(i, 2, [0, 1])
                onehot_pair(i, 1, 2)
                transpose_tile(i, 2, [2, 3])
                onehot_pair(i, 1, 3)
                transpose_tile(i, 2, [4])
                pairs_of_half(i, 1)

            pe.wait_ge(consts_made, 3)
            onehot_pair(0, 0, 0)
            onehot_pair(0, 0, 1)
            transpose_tile(0, 0)
            onehot_pair(0, 0, 2)
            onehot_pair(0, 0, 3)
            pe.wait_ge(pad_set, 1)
            pairs_of_half(0, 0)
            second_half(0)
            pe.wait_ge(weights_low, 3)
            with pe.Fori(1, BLOCKS) as i:
                onehot_pair(i, 0, 0, [0])
                bottom_back(i - 1)
                relayout(i - 1, [0])
                onehot_pair(i, 0, 0, [1])
                relayout(i - 1, [1, 2])
                onehot_pair(i, 0, 0, [2])
                relayout(i - 1, [3, 4])
                onehot_pair(i, 0, 0, [3])
                relayout(i - 1, [5, 6])
                onehot_pair(i, 0, 1, [0])
                pairs_back(i - 1, [0, 1])
                onehot_pair(i, 0, 1, [1])
                pairs_back(i - 1, [2])
                onehot_pair(i, 0, 1, [2, 3])
                layer1(i - 1)
                transpose_tile(i, 0, [0, 1, 2])
                layer2(i - 1, 0, [0, 1])
                transpose_tile(i, 0, [3])
                layer2(i - 1, 0, [2, 3])
                transpose_tile(i, 0, [4])
                layer2(i - 1, 1)
                onehot_pair(i, 0, 2)
                onehot_pair(i, 0, 3)
                layer3(i - 1)
                pairs_of_half(i, 0)
                second_half(i)
                pe.wait_ge(dense_act, read_by("act", DENSE) * i)
            bottom_back(BLOCKS - 1)
            relayout(BLOCKS - 1, range(RG))
            pairs_back(BLOCKS - 1, range(3))
            layer1(BLOCKS - 1)
            layer2(BLOCKS - 1, 0)
            layer2(BLOCKS - 1, 1)
            layer3(BLOCKS - 1)


def kernel(**inputs):
    import numpy as _np
    import concourse.bacc as _bacc
    from concourse import mybir as _mybir
    from concourse.bass_utils import run_bass_kernel_spmd as _run

    nc = _bacc.Bacc("TRN2", target_bir_lowering=False, num_devices=1)
    tables = [_np.asarray(inputs[f"tbl_{f}"]) for f in range(FEATURES)]
    ids = _np.asarray(inputs["ids"])
    w1 = _np.asarray(inputs["W_top1"])
    gathered, onehot = slots([t.shape[0] for t in tables])
    layouts = {
        "bottom": _np.asarray(inputs["r_bottom_mlp_out"]),
        "ids": ids,
        "ids_onehot": ids[:, onehot].T,
        "w_bottom_a": w1[0:D],
        "w_pairs": w1[pair_rows(gathered + onehot)],
        "w_bottom_b": w1[D + PAIRS:],
        "b1": _np.asarray(inputs["b_top1"]).reshape(H1 // 128, 128).T,
        "w2": _np.asarray(inputs["W_top2"]),
        "b2": _np.asarray(inputs["b_top2"]).reshape(H2 // 128, 128).T,
        "w3": _np.asarray(inputs["W_top3"]).reshape(H2 // 128, 128).T,
    }
    arrays, args = {}, {}

    def operand(name, a):
        a = _np.ascontiguousarray(a)
        arrays[name + "_dram"] = a
        return nc.dram_tensor(name + "_dram", a.shape, _mybir.dt.from_np(a.dtype), kind="ExternalInput").ap()

    for name, a in layouts.items():
        args[name] = operand(name, a)
    args["tables"] = [operand(f"tbl_{f}", t) for f, t in enumerate(tables)]
    args["out"] = nc.dram_tensor("y_dram", (BATCH, 1), _mybir.dt.float32, kind="ExternalOutput").ap()
    dlrm_tower(nc, **args)
    r = _run(nc, [arrays], core_ids=[0])
    return r.results[0]["y_dram"]
```

```python
import concourse.bass as bass
from concourse import mybir
from contextlib import ExitStack

BATCH, FEATURES, D = 2048, 27, 128
SMALL_VOCAB = 1000
ONEHOT_TABLES = 8
BLOCK, HALF, TILE = 512, 256, 128
BLOCKS, TILES = BATCH // BLOCK, BLOCK // TILE
PAD = 32
GROUP = 4
JG = BLOCK // GROUP
PG = FEATURES - 1
PAIRS = FEATURES * PG // 2
CHUNK = PAIRS // 3
H1, H2 = 512, 256
HIGH, LOW = 0, 1


def slots(vocabs):
    onehot = [f for f in range(FEATURES) if vocabs[f] == SMALL_VOCAB][:ONEHOT_TABLES]
    gathered = [f for f in range(FEATURES) if f not in onehot]
    return gathered, onehot


def pair_rows(order):
    rows = []
    for f in range(1, FEATURES):
        for g in range(f):
            a, b = max(order[f], order[g]), min(order[f], order[g])
            rows.append(D + a * (a - 1) // 2 + b)
    return rows


def dlrm_tower(nc, bottom, ids, ids_onehot, tables, w_bottom_a, w_pairs, w_bottom_b, b1, w2, b2, w3, out):
    fp32, fp32r, i32 = mybir.dt.float32, mybir.dt.float32r, mybir.dt.int32
    ALU = mybir.AluOpType
    ACT = mybir.ActivationFunctionType

    gathered, onehot = slots([t.shape[0] for t in tables])
    NG, NO = len(gathered), len(onehot)
    VB = 8
    VP = SMALL_VOCAB // VB
    VP_A = VP // 16 * 16
    FQ = 4
    TQ = (NG + FQ - 1) // FQ
    RAWS = 5
    OP = NO // 2
    assert NO % 2 == 0 and VP <= 128

    def hot_use(half, p, bank):
        return [(("hot", half, p), bank)]

    def tile_use(t, first_bank):
        return [(("tile", t, u), (first_bank + u) % 2) for u in range(TQ)]

    first, inner = tile_use(2, 0)[:2], [(use, (1 - b)) for use, b in tile_use(2, 0)[2:]]
    build_plan = (hot_use(0, 0, 0) + hot_use(0, 1, 1) + tile_use(0, 0) + hot_use(0, 2, 1) + hot_use(0, 3, 0)
                  + tile_use(1, 1) + first
                  + inner[0:1] + hot_use(1, 0, 0) + inner[1:2] + hot_use(1, 1, 1) + inner[2:3] + hot_use(1, 2, 0)
                  + hot_use(1, 3, 1) + tile_use(3, 0))
    BUILD_ORDER = [use for use, _ in build_plan]
    BUILD_BANK = [bank for _, bank in build_plan]
    BUILDS = len(BUILD_ORDER)
    assert OP == 4 and TQ == 5

    def bank_slots(u):
        return range(u * FQ, min((u + 1) * FQ, NG))

    def nth(*use):
        return BUILD_ORDER.index(use)

    def tile_end(t):
        return nth("tile", t, TQ - 1) + 1

    def hot_end(half, p):
        return nth("hot", half, p) + 1

    HOTS = 2 * 2 * NO
    GB = 8
    GU = TILE // GROUP // GB
    GRAMS = TILES * GU
    GC = GROUP * PG
    GR = (GROUP - 1) * PAD + PG
    RB = 4
    RG = (PG + RB - 1) // RB
    M1, M2 = H1 // 128, H2 // 128
    USE_R, USE_G, USE_X = 0, 1, 1 + RG
    USE_1 = USE_X + 3
    USE_2 = USE_1 + M1
    USE_Y = USE_2 + M2
    DENSE = USE_Y + 1
    reader = ["dve"] + ["dve" if u % 2 == 0 else "act" for u in range(RG)] + ["dve"] * 3 + ["dve"] * M1 + ["act"] * M2 + ["act"]
    HIGHS = 1 + 3 + M1
    assert DENSE % 2 == 0 and len(reader) == DENSE

    def read_by(engine, upto):
        return reader[:upto].count(engine)

    ctx = ExitStack()
    with ctx:
        def sb(name, shape, dt):
            return ctx.enter_context(nc.sbuf_tensor(name, shape, dt))

        def sem(name):
            return ctx.enter_context(nc.semaphore(name))

        KIB = 1024
        arena_at = (nc.sbuf_base + 31) // 32 * 32
        arena = sb("arena", [128, 20 * KIB // 4], fp32)

        weight_arena_at = (nc.sbuf_base + 31) // 32 * 32
        weight_arena = sb("weight_arena", [128, 12 * KIB // 4], fp32)

        def in_arena(name, shape, dt, at):
            return nc.alloc_sbuf_tensor_at(name, shape, dt, offset=arena_at + at)

        def in_weight_arena(name, shape, dt, at):
            return nc.alloc_sbuf_tensor_at(name, shape, dt, offset=weight_arena_at + at)

        raw = in_arena("raw", [128, RAWS, VB * D], fp32, 0)
        w1p_raw = in_weight_arena("w1p_raw", [CHUNK, 3, H1], fp32, 0)
        w1b_raw = in_weight_arena("w1b_raw", [128, H1], fp32, 6 * KIB)
        w2_raw = in_weight_arena("w2_raw", [128, M1, H2], fp32, 8 * KIB)
        pairT = in_weight_arena("pairT", [CHUNK, 2, 3, BLOCK], fp32r, 0)
        gram = in_arena("gram", [GR, PG, JG], fp32, 0)
        h1 = in_arena("h1", [128, 2, M1, BLOCK], fp32r, 0)
        h2 = in_arena("h2", [128, M2, BLOCK], fp32, 16 * KIB)

        embT = sb("embT", [128, HALF, PAD], fp32)
        rows = sb("rows", [128, 2, NG * D], fp32)
        idx = sb("idx", [128, TILES, FEATURES], i32)
        table = sb("table", [128, NO, 2, VB * D], fp32r)
        id_raw = sb("id_raw", [128, 2, 2, HALF], i32)
        hot = sb("hot", [128, 2, 2, VB // 2, HALF], fp32r)
        vocab_i = sb("vocab_i", [128, VB], i32)
        vocab = sb("vocab", [128, VB], fp32)
        ident = sb("ident", [128, 128], fp32)
        packed = sb("packed", [128, GROUP, PAIRS], fp32)
        w1b_more = packed[:, 0:2, 0:H1 // 2]
        bot = sb("bot", [128, GROUP, D], fp32)
        botT = sb("botT", [128, 2, BLOCK], fp32r)
        w1p = sb("w1p", [CHUNK, 2, 3, H1], fp32r)
        w1b = sb("w1b", [128, 2, H1], fp32r)
        w2s = sb("w2s", [128, 2, M1, H2], fp32r)
        w3s = sb("w3s", [128, M2], fp32)
        b1s = sb("b1s", [128, M1], fp32)
        b2s = sb("b2s", [128, M2], fp32)
        y = sb("y", [128, GROUP], fp32)

        ps_build = [ctx.enter_context(nc.psum_tensor(f"ps_build{i}", [128, 512], fp32)) for i in range(2)]
        ps_gram = [ctx.enter_context(nc.psum_tensor(f"ps_gram{i}", [128, 1024], fp32)) for i in range(2)]
        ps_dense = [ctx.enter_context(nc.psum_tensor(f"ps_dense{i}", [128, 512], fp32)) for i in range(2)]

        consts_made = sem("consts_made")
        weights_in = sem("weights_in")
        idx_in = [sem(f"idx_in{t}") for t in range(TILES)]
        rows_in = [[sem(f"rows_in{s}_{u}") for u in range(TQ)] for s in range(2)]
        raw_in = [sem(f"raw_in{s}") for s in range(RAWS)]
        id_in = [sem(f"id_in{s}") for s in range(2)]
        bot_in = sem("bot_in")
        pad_set = sem("pad_set")
        table_high = sem("table_high")
        table_low = sem("table_low")
        w1b_added = sem("w1b_added")
        weights_high = sem("weights_high")
        weights_low = sem("weights_low")
        loads_begun = sem("loads_begun")
        gathers_begun = sem("gathers_begun")
        hot_made = sem("hot_made")
        hot_used = sem("hot_used")
        built = sem("built")
        emb_done = sem("emb_done")
        grammed = sem("grammed")
        gram_dve = sem("gram_dve")
        gram_act = sem("gram_act")
        densed = sem("densed")
        relu_done = sem("relu_done")
        high_made = sem("high_made")
        dense_dve = sem("dense_dve")
        dense_act = sem("dense_act")
        dve_step = sem("dve_step")
        out_done = sem("out_done")
        dense_read = {"dve": dense_dve, "act": dense_act}
        WEIGHT_LOADS = 7
        FIRST_STEPS = [(0, (0, 1), 0), (1, (0,), 1), (1, (1,), 2), (2, (0,), 3), (2, (1,), 4), (3, (0, 1), None)]
        def second_steps(half):
            return [(u, (0, 1), u - 1 if half == 0 and u in (1, 2) else None) for u in range(GU)]

        def gram_pieces(t, u, k):
            rows_k = slice(PAD * k, min(PAD * (k + 1), GR))
            src = ps_gram[u % 2][rows_k, :].rearrange("p (h c) -> p h c", h=2)
            src = src[:, :, 0:GB // 2 * GC].rearrange("p h (g c) -> p c h g", g=GB // 2)[:, k * PG:(k + 1) * PG]
            j = (t * GU + u) * GB
            dst = gram[rows_k, :, j:j + GB].rearrange("p f (h g) -> p f h g", h=2)
            return dst, src

        def pack_pieces(u):
            for n in range(u * RB, min((u + 1) * RB, PG)):
                f = n + 1
                at = f * (f - 1) // 2
                src = ps_dense[(USE_G + u) % 2][:, (n % RB) * 128:(n % RB + 1) * 128]
                yield packed[:, :, at:at + f], src.rearrange("p (k g) -> p k g", k=GROUP)[:, :, 0:f]

        block = ctx.enter_context(nc.Block())

        @block.sync
        def _(sp):
            def load_idx(at, t):
                sp.dma_start(idx[:, t, :], ids[bass.ds(at, BLOCK), :][t * TILE:(t + 1) * TILE, :]).then_inc(idx_in[t], 16)

            def load_ids(at, n):
                half, p = n // OP, n % OP
                src = ids_onehot[2 * p:2 * p + 2, bass.ds(at, BLOCK)][:, half * HALF:(half + 1) * HALF]
                sp.dma_start(id_raw[:, n % 2, :, :], src.unsqueeze(0).broadcast_to([128, 2, HALF])).then_inc(id_in[n % 2], 16)

            def load_bottom(at):
                src = bottom[bass.ds(at, BLOCK), :].rearrange("(j k) d -> j k d", k=GROUP)
                sp.dma_start(bot[:, :, :], src).then_inc(bot_in, 16)

            def load_table(q):
                src = tables[onehot[q]].rearrange("(p v) d -> p (v d)", v=VB)
                sp.dma_start(raw[0:VP_A, q % RAWS, :], src[0:VP_A, :]).then_inc(raw_in[q % RAWS], 16)
                sp.dma_start(raw[VP_A:VP, q % RAWS, :], src[VP_A:VP, :]).then_inc(raw_in[q % RAWS], 16)

            def store(i, at):
                sp.wait_ge(dense_act, read_by("act", DENSE) * (i + 1))
                sp.sem_inc(loads_begun, 1)
                sp.dma_start(out[bass.ds(at, BLOCK), :].rearrange("(j k) o -> j (k o)", k=GROUP), y[:, :]).then_inc(out_done, 16)

            load_idx(0, 0)
            load_ids(0, 0)
            load_table(0)
            load_table(1)
            load_ids(0, 1)
            load_table(2)
            load_table(3)
            load_idx(0, 1)
            load_table(4)
            load_idx(0, 2)
            load_idx(0, 3)
            for q in range(RAWS, NO):
                sp.wait_ge(table_low, q - RAWS + 1)
                load_table(q)
            load_bottom(0)
            for n in range(2, 2 * OP):
                sp.wait_ge(hot_made, 4 * (n - 1))
                load_ids(0, n)
            with sp.Fori(1, BLOCKS) as i:
                at = sp.snap(i * BLOCK)
                before = sp.snap(i * BLOCK - BLOCK)

                def next_idx(t):
                    for u in range(TQ):
                        sp.wait_ge(rows_in[t % 2][u], 16 * len(bank_slots(u)) * (2 * i - 1 + t // 2))
                        sp.sem_inc(loads_begun, 1)
                    load_idx(at, t)

                def next_ids(n):
                    sp.wait_ge(hot_made, HOTS * i + 4 * (n - 1))
                    sp.sem_inc(loads_begun, 1)
                    load_ids(at, n)

                next_idx(0)
                next_idx(1)
                next_idx(2)
                next_ids(0)
                next_ids(1)
                next_idx(3)
                sp.wait_ge(densed, DENSE * (i - 1) + USE_R + 1)
                sp.sem_inc(loads_begun, 1)
                load_bottom(at)
                for n in range(2, OP + 1):
                    next_ids(n)
                store(i - 1, before)
                for n in range(OP + 1, 2 * OP):
                    next_ids(n)
            store(BLOCKS - 1, BATCH - BLOCK)
            sp.wait_ge(out_done, 16 * BLOCKS)

        @block.gpsimd
        def _(pool):
            nc.gpsimd.iota(vocab_i[:, :], pattern=[[1, VB]], base=0, channel_multiplier=VB).then_inc(consts_made, 1)
            nc.gpsimd.memset(ident[:, :], 0.0).then_inc(consts_made, 1)
            pool.wait_ge(consts_made, 2)
            nc.gpsimd.affine_select(out=ident[:, :], in_=ident[:, :], compare_op=ALU.not_equal, fill=1.0, base=0,
                                    pattern=[[-1, 128]], channel_multiplier=1).then_inc(consts_made, 1)

            def gather(i, t):
                pool.wait_ge(idx_in[t], 16 * (i + 1))
                for u in range(TQ):
                    if t >= 2:
                        pool.wait_ge(built, BUILDS * i + nth("tile", t - 2, u) + 1)
                    elif not (isinstance(i, int) and i == 0):
                        pool.wait_ge(built, BUILDS * (i - 1) + nth("tile", t + 2, u) + 1)
                    pool.sem_inc(gathers_begun, 1)
                    for s in bank_slots(u):
                        f = gathered[s]
                        nc.gpsimd.indirect_dma_start(
                            rows[:, t % 2, s * D:(s + 1) * D], None, tables[f],
                            bass.IndirectOffsetOnAxis(idx[:, t, f:f + 1], 0)).then_inc(rows_in[t % 2][u], 16)

            for t in range(TILES):
                gather(0, t)
            with pool.Fori(1, BLOCKS) as i:
                for t in range(TILES):
                    gather(i, t)

        @block.vector
        def _(dve):
            def low_part(dst, whole, high):
                return nc.vector.tensor_tensor(dst, whole, high.bitcast(fp32), ALU.subtract)

            def split_table(q):
                dve.wait_ge(table_high, q + 1)
                low_part(table[0:VP, q, LOW, :], raw[0:VP, q % RAWS, :], table[0:VP, q, HIGH, :]).then_inc(table_low, 1)

            def make_hot(i, half, p, parts=range(4)):
                n = half * OP + p
                first = isinstance(i, int) and i == 0
                if 0 in parts:
                    dve.wait_ge(id_in[n % 2], 16 * (OP * i + n // 2 + 1))
                for part in parts:
                    q, v0 = part // 2, part % 2
                    if n > 0 and part < 3:
                        dve.wait_ge(hot_used, 3 * (2 * OP * i + n - 1) + part + 1)
                    elif n > 0:
                        dve.wait_ge(built, BUILDS * i + hot_end((n - 1) // OP, (n - 1) % OP))
                    elif not first and part < 3:
                        dve.wait_ge(hot_used, 3 * (2 * OP * i - 1) + part + 1)
                    elif not first:
                        dve.wait_ge(built, BUILDS * (i - 1) + hot_end(1, OP - 1))
                    for v in range(VB // 2):
                        row = v0 * VB // 2 + v
                        last = nc.vector.tensor_scalar(hot[0:VP, q, v0, v, :], id_raw[0:VP, n % 2, q, :],
                                                       vocab[0:VP, row:row + 1], None, ALU.is_equal)
                    last.then_inc(hot_made, 1)

            def empty_gram(i, t, u):
                dve.wait_ge(grammed, GRAMS * i + t * GU + u + 1)
                for k in (0, 1):
                    last = nc.vector.tensor_copy(*gram_pieces(t, u, k))
                last.then_inc(gram_dve, 1)

            def pairs_of_half(i, half, next_hot):
                for n in range(2 * GU):
                    empty_gram(i, 2 * half + n // GU, n % GU)
                    if next_hot and n % 2:
                        make_hot(*next_hot, [n // 2])

            def dense_low(i, w, high_n, dst, high, rows_used=128):
                dve.wait_ge(high_made, HIGHS * i + high_n + 1)
                low_part(dst, ps_dense[w % 2][0:rows_used, :], high).then_inc(dense_dve, 1)

            def pack(i, u):
                dve.wait_ge(densed, DENSE * i + USE_G + u + 1)
                for dst, src in pack_pieces(u):
                    last = nc.vector.tensor_copy(dst, src)
                last.then_inc(dense_dve, 1)

            def dense(i, hots):
                for u in range(0, RG, 2):
                    pack(i, u)
                    hots(1, u // 2)
                for c in range(3):
                    dense_low(i, USE_X + c, 1 + c, pairT[:, LOW, c, :], pairT[:, HIGH, c, :], CHUNK)
                hots(2, 0)
                for m in range(M1):
                    if m < 3:
                        hots(2, m + 1)
                    dense_low(i, USE_1 + m, 4 + m, h1[:, LOW, m, :], h1[:, HIGH, m, :])

            def add_w1b():
                dve.wait_ge(weights_in, 16 * WEIGHT_LOADS)
                halves = w1b_raw[:, :].rearrange("p (a b) -> p a b", a=2)
                nc.vector.tensor_tensor(halves, halves, w1b_more, ALU.add).then_inc(w1b_added, 1)

            def split_weights():
                dve.wait_ge(weights_high, 3)
                low_part(w1p[:, LOW, :, :], w1p_raw[:, :, :], w1p[:, HIGH, :, :]).then_inc(weights_low, 1)
                low_part(w1b[:, LOW, :], w1b_raw[:, :], w1b[:, HIGH, :]).then_inc(weights_low, 1)
                low_part(w2s[:, LOW, :, :], w2_raw[:, :, :], w2s[:, HIGH, :, :]).then_inc(weights_low, 1)

            def block_work(i, more):
                if not (isinstance(i, int) and i == 0):
                    make_hot(i, 0, 3)
                pairs_of_half(i, 0, (i, 1, 0))
                for p in range(1, OP):
                    make_hot(i, 1, p)
                if isinstance(i, int) and i == 0:
                    add_w1b()
                    split_weights()
                dense_low(i, USE_R, 0, botT[:, LOW, :], botT[:, HIGH, :])
                pairs_of_half(i, 1, (i + 1, 0, 0) if more else None)

            nc.vector.memset(embT[:, :, FEATURES:PAD], 0.0).then_inc(pad_set, 1)
            dve.wait_ge(consts_made, 1)
            nc.vector.tensor_copy(vocab[:, :], vocab_i[:, :]).then_inc(dve_step, 1)
            dve.wait_ge(dve_step, 1)
            make_hot(0, 0, 0)
            split_table(0)
            split_table(1)
            for p in range(1, OP):
                make_hot(0, 0, p, [0])
                split_table(2 * p)
                make_hot(0, 0, p, [1])
                split_table(2 * p + 1)
                make_hot(0, 0, p, [2, 3])
            block_work(0, True)
            with dve.Fori(1, BLOCKS - 1) as i:
                dense(i - 1, lambda p, part: make_hot(i, 0, p, [part]))
                block_work(i, True)
            dense(BLOCKS - 2, lambda p, part: make_hot(BLOCKS - 1, 0, p, [part]))
            block_work(BLOCKS - 1, False)
            dense(BLOCKS - 1, lambda p, part: None)

        @block.scalar
        def _(act):
            def load_weights():
                for dst, src in ((w1b_raw[:, :], w_bottom_a), (w1b_more, w_bottom_b.rearrange("p (a b) -> p a b", a=2)),
                                 (w1p_raw[:, :, :], w_pairs.rearrange("(c p) h -> p c h", c=3)),
                                 (w2_raw[:, :, :], w2.rearrange("(c p) h -> p c h", p=128)),
                                 (w3s[:, :], w3), (b1s[:, :], b1), (b2s[:, :], b2)):
                    act.dma_start(dst, src).then_inc(weights_in, 16)

            def split_table(q):
                act.wait_ge(raw_in[q % RAWS], 32 * (q // RAWS + 1))
                nc.scalar.copy(table[0:VP, q, HIGH, :], raw[0:VP, q % RAWS, :]).then_inc(table_high, 1)

            def split_weights():
                act.wait_ge(weights_in, 16 * WEIGHT_LOADS)
                nc.scalar.copy(w1p[:, HIGH, :, :], w1p_raw[:, :, :]).then_inc(weights_high, 1)
                nc.scalar.copy(w2s[:, HIGH, :, :], w2_raw[:, :, :]).then_inc(weights_high, 1)
                act.wait_ge(w1b_added, 1)
                nc.scalar.copy(w1b[:, HIGH, :], w1b_raw[:, :]).then_inc(weights_high, 1)

            def emb_hot(i, half, p):
                s = nth("hot", half, p)
                act.wait_ge(built, BUILDS * i + s + 1)
                nc.scalar.copy(embT[:, :, NG + 2 * p:NG + 2 * p + 2],
                               ps_build[BUILD_BANK[s]][:, :].rearrange("p (q b) -> p b q", q=2)).then_inc(emb_done, 1)

            def emb_tile(i, t, banks=range(TQ)):
                for u in banks:
                    s = nth("tile", t, u)
                    n = min(FQ, NG - u * FQ)
                    act.wait_ge(built, BUILDS * i + s + 1)
                    src = ps_build[BUILD_BANK[s]][:, 0:n * 128].rearrange("p (f b) -> p b f", f=n)
                    b = t % 2 * TILE
                    nc.scalar.copy(embT[:, b:b + TILE, u * FQ:u * FQ + n], src).then_inc(emb_done, 1)

            def empty_gram(i, t, u):
                act.wait_ge(grammed, GRAMS * i + t * GU + u + 1)
                for k in (2, 3):
                    last = nc.scalar.copy(*gram_pieces(t, u, k))
                last.then_inc(gram_act, 1)

            def pairs_of_half(i, half, dense=None):
                t = 2 * half
                for u, banks, lookups in FIRST_STEPS:
                    if 1 in banks:
                        empty_gram(i, t, u)
                    if lookups is not None:
                        emb_tile(i, t + 1, [lookups])
                    if u == 0 and dense is not None:
                        layer3(dense)
                for u, banks, lookups in second_steps(half):
                    empty_gram(i, t + 1, u)
                    if lookups is not None:
                        emb_tile(i, t + 2, [lookups])

            def dense_high(i, w, dst, rows_used=128):
                act.wait_ge(densed, DENSE * i + w + 1)
                nc.scalar.copy(dst, ps_dense[w % 2][0:rows_used, :]).then_inc(high_made, 1)

            def relayout(i):
                for u in range(RG):
                    if reader[USE_G + u] == "act":
                        act.wait_ge(densed, DENSE * i + USE_G + u + 1)
                        for dst, src in pack_pieces(u):
                            last = nc.scalar.copy(dst, src)
                        last.then_inc(dense_act, 1)

            def pair_highs(i):
                for c in range(3):
                    dense_high(i, USE_X + c, pairT[:, HIGH, c, :], CHUNK)

            def layer1(i, between=None):
                for m in range(M1):
                    if between is not None:
                        emb_tile(between, 0, [m])
                    w = USE_1 + m
                    act.wait_ge(densed, DENSE * i + w + 1)
                    nc.scalar.activation(ps_dense[w % 2][:, :], ps_dense[w % 2][:, :], ACT.Relu,
                                         bias=b1s[:, m:m + 1]).then_inc(relu_done, 1)
                    act.wait_ge(relu_done, M1 * i + m + 1)
                    nc.scalar.copy(h1[:, HIGH, m, :], ps_dense[w % 2][:, :]).then_inc(high_made, 1)

            def layer2(i, m):
                w = USE_2 + m
                act.wait_ge(densed, DENSE * i + w + 1)
                nc.scalar.activation(h2[:, m, :], ps_dense[w % 2][:, :], ACT.Relu,
                                     bias=b2s[:, m:m + 1]).then_inc(dense_act, 1)

            def layer3(i):
                act.wait_ge(densed, DENSE * i + USE_Y + 1)
                nc.scalar.copy(y[:, :], ps_dense[USE_Y % 2][:, 0:GROUP]).then_inc(dense_act, 1)

            def second_half(i):
                for p in range(OP - 1):
                    emb_tile(i, 2, [p + 2])
                    emb_hot(i, 1, p)
                    if isinstance(i, int) and p == 1:
                        split_weights()
                emb_hot(i, 1, OP - 1)
                dense_high(i, USE_R, botT[:, HIGH, :])
                pairs_of_half(i, 1)

            for q in range(NO):
                split_table(q)
                if q == 3:
                    emb_hot(0, 0, 0)
                if q == 5:
                    emb_hot(0, 0, 1)
            load_weights()
            emb_tile(0, 0)
            emb_hot(0, 0, 2)
            emb_hot(0, 0, 3)
            pairs_of_half(0, 0)
            second_half(0)
            with act.Fori(1, BLOCKS) as i:
                relayout(i - 1)
                emb_hot(i, 0, 0)
                pair_highs(i - 1)
                emb_hot(i, 0, 1)
                layer1(i - 1, i)
                emb_tile(i, 0, [4])
                layer2(i - 1, 0)
                emb_hot(i, 0, 2)
                emb_hot(i, 0, 3)
                layer2(i - 1, 1)
                pairs_of_half(i, 0, i - 1)
                second_half(i)
                act.wait_ge(out_done, 16 * i)
            relayout(BLOCKS - 1)
            pair_highs(BLOCKS - 1)
            layer1(BLOCKS - 1)
            layer2(BLOCKS - 1, 0)
            layer2(BLOCKS - 1, 1)
            layer3(BLOCKS - 1)

        @block.tensor
        def _(pe):
            def build_bank(i, s):
                before = [n for n in range(s) if BUILD_BANK[n] == BUILD_BANK[s]]
                if before:
                    pe.wait_ge(emb_done, BUILDS * i + before[-1] + 1)
                elif not (isinstance(i, int) and i == 0):
                    last = max(n for n in range(BUILDS) if BUILD_BANK[n] == BUILD_BANK[s])
                    pe.wait_ge(emb_done, BUILDS * (i - 1) + last + 1)
                return ps_build[BUILD_BANK[s]]

            def dense_bank(i, w):
                if w >= 2:
                    e = reader[w - 2]
                    pe.wait_ge(dense_read[e], read_by(e, DENSE) * i + read_by(e, w - 1))
                return ps_dense[w % 2]

            def onehot_pair(i, half, p, parts=range(4)):
                n = half * OP + p
                s = nth("hot", half, p)
                bank = build_bank(i, s) if 0 in parts else ps_build[BUILD_BANK[s]]
                for part in parts:
                    q, v0 = part // 2, part % 2
                    if isinstance(i, int) and i == 0 and half == 0 and v0 == 0:
                        pe.wait_ge(table_low, 2 * p + q + 1)
                    pe.wait_ge(hot_made, HOTS * i + 4 * n + part + 1)
                    for v in range(VB // 2):
                        row = (v0 * VB // 2 + v) * D
                        for bits in (HIGH, LOW):
                            last = nc.tensor.matmul(bank[:, q * HALF:(q + 1) * HALF],
                                                    table[0:VP, 2 * p + q, bits, row:row + D],
                                                    hot[0:VP, q, v0, v, :], start=(v0 == v == bits == 0),
                                                    stop=(v0 == 1 and v == VB // 2 - 1 and bits == LOW))
                    last.then_inc(hot_used if part < 3 else built, 1)

            def transpose_tile(i, t, banks=range(TQ)):
                for u in banks:
                    pe.wait_ge(rows_in[t % 2][u], 16 * len(bank_slots(u)) * (2 * i + t // 2 + 1))
                    bank = build_bank(i, nth("tile", t, u))
                    for f, s in enumerate(bank_slots(u)):
                        last = nc.tensor.transpose(bank[:, f * 128:(f + 1) * 128], rows[:, t % 2, s * D:(s + 1) * D],
                                                   ident[:, :])
                    last.then_inc(built, 1)

            def pair_products(i, t, u, banks):
                v = t * GU + u
                if 0 in banks:
                    if u == 0:
                        pe.wait_ge(emb_done, BUILDS * i + max(tile_end(t), hot_end(t // 2, OP - 1)))
                    if v >= 2:
                        pe.wait_ge(gram_dve, GRAMS * i + v - 1)
                        pe.wait_ge(gram_act, GRAMS * i + v - 1)
                for b in banks:
                    for g in range(GB // 2):
                        at = t % 2 * TILE + (u * GB + b * GB // 2 + g) * GROUP
                        c = b * 512 + g * GC
                        last = nc.tensor.matmul(ps_gram[u % 2][0:GR, c:c + GC],
                                                embT[:, at:at + GROUP, :].rearrange("p k g -> p (k g)")[:, 0:GR],
                                                embT[:, at:at + GROUP, 1:FEATURES], start=True, stop=True)
                if 1 in banks:
                    last.then_inc(grammed, 1)

            def bottom_back(i):
                pe.wait_ge(bot_in, 16 * (i + 1))
                bank = dense_bank(i, USE_R)
                for k in range(GROUP):
                    last = nc.tensor.transpose(bank[:, k * JG:(k + 1) * JG], bot[:, k, :], ident[:, :])
                last.then_inc(densed, 1)

            def relayout(i, banks):
                if 0 in banks:
                    pe.wait_ge(gram_dve, GRAMS * (i + 1))
                    pe.wait_ge(gram_act, GRAMS * (i + 1))
                for u in banks:
                    bank = dense_bank(i, USE_G + u)
                    for n in range(u * RB, min((u + 1) * RB, PG)):
                        last = nc.tensor.transpose(bank[:, (n % RB) * 128:(n % RB) * 128 + GR], gram[0:GR, n, :],
                                                   ident[0:GR, 0:GR])
                    last.then_inc(densed, 1)

            def wait_dense(i, upto):
                for e in ("dve", "act"):
                    pe.wait_ge(dense_read[e], read_by(e, DENSE) * i + read_by(e, upto))

            def pairs_back(i, chunks):
                if 0 in chunks:
                    wait_dense(i, USE_X)
                for c in chunks:
                    bank = dense_bank(i, USE_X + c)
                    for k in range(GROUP):
                        last = nc.tensor.transpose(bank[0:CHUNK, k * JG:(k + 1) * JG],
                                                   packed[:, k, c * CHUNK:(c + 1) * CHUNK], ident[:, :])
                    last.then_inc(densed, 1)

            def split_product(bank, w, x, first=False, end=False):
                for m, (a, b) in enumerate(((HIGH, HIGH), (HIGH, LOW), (LOW, HIGH))):
                    last = nc.tensor.matmul(bank[:, :], w(a), x(b), start=(first and m == 0), stop=(end and m == 2))
                return last

            def layer1(i, between=None):
                for m in range(M1):
                    if between is not None:
                        transpose_tile(between, 0, [m])
                    bank = dense_bank(i, USE_1 + m)
                    cols = slice(m * 128, (m + 1) * 128)
                    if m == 0:
                        wait_dense(i, USE_G)
                    split_product(bank, lambda a: w1b[:, a, cols], lambda b: botT[:, b, :], first=True)
                    if m == 0:
                        wait_dense(i, USE_1)
                    for c in range(3):
                        last = split_product(bank, lambda a: w1p[:, a, c, cols], lambda b: pairT[:, b, c, :], end=(c == 2))
                    last.then_inc(densed, 1)

            def layer2(i, m, chunks=range(M1)):
                w = USE_2 + m
                bank = dense_bank(i, w) if 0 in chunks else ps_dense[w % 2]
                cols = slice(m * 128, (m + 1) * 128)
                for c in chunks:
                    if m == 0:
                        wait_dense(i, USE_1 + c + 1)
                    last = split_product(bank, lambda a: w2s[:, a, c, cols], lambda b: h1[:, b, c, :],
                                         first=(c == 0), end=(c == M1 - 1))
                if M1 - 1 in chunks:
                    last.then_inc(densed, 1)

            def layer3(i):
                wait_dense(i, USE_Y)
                bank = dense_bank(i, USE_Y)
                for k in range(GROUP):
                    for c in range(M2):
                        last = nc.tensor.matmul(bank[:, k:k + 1], h2[:, c, k * JG:(k + 1) * JG], w3s[:, c:c + 1],
                                                start=(c == 0), stop=(c == M2 - 1))
                last.then_inc(densed, 1)

            def pairs_of_half(i, half, dense=None):
                t = 2 * half
                for u, banks, lookups in FIRST_STEPS:
                    pair_products(i, t, u, banks)
                    if lookups is not None:
                        transpose_tile(i, t + 1, [lookups])
                    if u == 0 and dense is not None:
                        layer3(dense)
                for u, banks, lookups in second_steps(half):
                    pair_products(i, t + 1, u, banks)
                    if lookups is not None:
                        transpose_tile(i, t + 2, [lookups])

            def second_half(i):
                for p in range(OP - 1):
                    onehot_pair(i, 1, p, [0, 1])
                    transpose_tile(i, 2, [p + 2])
                    onehot_pair(i, 1, p, [2, 3])
                onehot_pair(i, 1, OP - 1)
                if not isinstance(i, int):
                    pe.wait_ge(dense_act, read_by("act", DENSE) * i)
                bottom_back(i)
                pairs_of_half(i, 1)

            pe.wait_ge(consts_made, 3)
            onehot_pair(0, 0, 0)
            onehot_pair(0, 0, 1)
            transpose_tile(0, 0)
            onehot_pair(0, 0, 2)
            onehot_pair(0, 0, 3)
            pe.wait_ge(pad_set, 1)
            pairs_of_half(0, 0)
            second_half(0)
            pe.wait_ge(weights_low, 3)
            with pe.Fori(1, BLOCKS) as i:
                onehot_pair(i, 0, 0, [0])
                relayout(i - 1, [0])
                onehot_pair(i, 0, 0, [1])
                relayout(i - 1, [1, 2])
                onehot_pair(i, 0, 0, [2])
                relayout(i - 1, [3, 4])
                onehot_pair(i, 0, 0, [3])
                relayout(i - 1, [5, 6])
                onehot_pair(i, 0, 1, [0])
                pairs_back(i - 1, [0, 1])
                onehot_pair(i, 0, 1, [1])
                pairs_back(i - 1, [2])
                onehot_pair(i, 0, 1, [2, 3])
                layer1(i - 1, i)
                layer2(i - 1, 0, [0, 1, 2])
                transpose_tile(i, 0, [4])
                layer2(i - 1, 0, [3])
                onehot_pair(i, 0, 2)
                onehot_pair(i, 0, 3)
                layer2(i - 1, 1)
                pairs_of_half(i, 0, i - 1)
                second_half(i)
            relayout(BLOCKS - 1, range(RG))
            pairs_back(BLOCKS - 1, range(3))
            layer1(BLOCKS - 1)
            layer2(BLOCKS - 1, 0)
            layer2(BLOCKS - 1, 1)
            layer3(BLOCKS - 1)


def kernel(**inputs):
    import numpy as _np
    import concourse.bacc as _bacc
    from concourse import mybir as _mybir
    from concourse.bass_utils import run_bass_kernel_spmd as _run

    nc = _bacc.Bacc("TRN2", target_bir_lowering=False, num_devices=1)
    tables = [_np.asarray(inputs[f"tbl_{f}"]) for f in range(FEATURES)]
    ids = _np.asarray(inputs["ids"])
    w1 = _np.asarray(inputs["W_top1"])
    gathered, onehot = slots([t.shape[0] for t in tables])
    layouts = {
        "bottom": _np.asarray(inputs["r_bottom_mlp_out"]),
        "ids": ids,
        "ids_onehot": ids[:, onehot].T,
        "w_bottom_a": w1[0:D],
        "w_pairs": w1[pair_rows(gathered + onehot)],
        "w_bottom_b": w1[D + PAIRS:],
        "b1": _np.asarray(inputs["b_top1"]).reshape(H1 // 128, 128).T,
        "w2": _np.asarray(inputs["W_top2"]),
        "b2": _np.asarray(inputs["b_top2"]).reshape(H2 // 128, 128).T,
        "w3": _np.asarray(inputs["W_top3"]).reshape(H2 // 128, 128).T,
    }
    arrays, args = {}, {}

    def operand(name, a):
        a = _np.ascontiguousarray(a)
        arrays[name + "_dram"] = a
        return nc.dram_tensor(name + "_dram", a.shape, _mybir.dt.from_np(a.dtype), kind="ExternalInput").ap()

    for name, a in layouts.items():
        args[name] = operand(name, a)
    args["tables"] = [operand(f"tbl_{f}", t) for f, t in enumerate(tables)]
    args["out"] = nc.dram_tensor("y_dram", (BATCH, 1), _mybir.dt.float32, kind="ExternalOutput").ap()
    dlrm_tower(nc, **args)
    r = _run(nc, [arrays], core_ids=[0])
    return r.results[0]["y_dram"]
```

```python
import concourse.bass as bass
from concourse import mybir
from contextlib import ExitStack

BATCH, FEATURES, D = 2048, 27, 128
SMALL_VOCAB = 1000
ONEHOT_TABLES = 8
BLOCK, HALF, TILE = 512, 256, 128
TILES = BLOCK // TILE
HEAD, FULL = -1, BATCH // BLOCK - 1
LAST = FULL
BLOCKS = FULL + 2
PAD = 32
GROUP = 4
JG = BLOCK // GROUP
PG = FEATURES - 1
PAIRS = FEATURES * PG // 2
CHUNK = PAIRS // 3
H1, H2 = 512, 256
HIGH, LOW = 0, 1


def at_block(i, b):
    return isinstance(i, int) and i == b


def half_width(i):
    return at_block(i, HEAD) or at_block(i, LAST)


def before(i, per_block):
    return 0 if at_block(i, HEAD) else i * per_block + per_block // 2


def groups(i):
    return JG // 2 if half_width(i) else JG


def items(i):
    return GROUP * groups(i)


def slots(vocabs):
    onehot = [f for f in range(FEATURES) if vocabs[f] == SMALL_VOCAB][:ONEHOT_TABLES]
    gathered = [f for f in range(FEATURES) if f not in onehot]
    return gathered, onehot


def pair_rows(order):
    rows = []
    for f in range(1, FEATURES):
        for g in range(f):
            a, b = max(order[f], order[g]), min(order[f], order[g])
            rows.append(D + a * (a - 1) // 2 + b)
    return rows


def dlrm_tower(nc, bottom, ids, ids_onehot, tables, w_bottom_a, w_pairs, w_bottom_b, b1, w2, b2, w3, out):
    fp32, fp32r, i32 = mybir.dt.float32, mybir.dt.float32r, mybir.dt.int32
    ALU = mybir.AluOpType
    ACT = mybir.ActivationFunctionType

    gathered, onehot = slots([t.shape[0] for t in tables])
    NG, NO = len(gathered), len(onehot)
    VB = 8
    VP = SMALL_VOCAB // VB
    VP_A = VP // 16 * 16
    FQ = 4
    TQ = (NG + FQ - 1) // FQ
    RAWS = 5
    OP = NO // 2
    assert NO % 2 == 0 and VP <= 128

    def hot_use(half, p, bank):
        return [(("hot", half, p), bank)]

    def tile_use(t, first_bank):
        return [(("tile", t, u), (first_bank + u) % 2) for u in range(TQ)]

    first, inner = tile_use(2, 0)[:2], [(use, (1 - b)) for use, b in tile_use(2, 0)[2:]]
    build_plan = (hot_use(0, 0, 0) + hot_use(0, 1, 1) + tile_use(0, 0) + hot_use(0, 2, 1) + hot_use(0, 3, 0)
                  + tile_use(1, 1) + first
                  + inner[0:1] + hot_use(1, 0, 0) + inner[1:2] + hot_use(1, 1, 1) + inner[2:3] + hot_use(1, 2, 0)
                  + hot_use(1, 3, 1) + tile_use(3, 0))
    LATE_PAIRS = range(1, OP)
    tile0 = [(("tile", 0, u), 1) for u in range(TQ)]
    tile0[3] = (tile0[3][0], 0)
    last_plan = (tile0[0:2] + hot_use(0, 0, 0) + tile0[2:] + hot_use(0, 1, 0) + hot_use(0, 2, 1) + hot_use(0, 3, 0)
                 + tile_use(1, 1))
    BUILDS = len(build_plan)
    assert OP == 4 and TQ == 5

    def plan(i):
        return last_plan if at_block(i, LAST) else build_plan

    def bank_slots(u):
        return range(u * FQ, min((u + 1) * FQ, NG))

    def nth(i, *use):
        return [u for u, _ in plan(i)].index(use)

    def bank_of(i, s):
        return plan(i)[s][1]

    def tile_end(i, t):
        return nth(i, "tile", t, TQ - 1) + 1

    def hot_end(i, half, p):
        return nth(i, "hot", half, p) + 1

    HOTS = 2 * 2 * NO
    GB = 8
    GU = TILE // GROUP // GB
    GRAMS = TILES * GU
    GC = GROUP * PG
    GR = (GROUP - 1) * PAD + PG
    RB = 4
    RG = (PG + RB - 1) // RB
    M1, M2 = H1 // 128, H2 // 128
    USE_R, USE_G, USE_X = 0, 1, 1 + RG
    USE_1 = USE_X + 3
    USE_2 = USE_1 + M1
    USE_Y = USE_2 + M2
    DENSE = USE_Y + 1
    reader = ["dve"] + ["dve" if u % 2 == 0 else "act" for u in range(RG)] + ["dve"] * 3 + ["dve"] * M1 + ["act"] * M2 + ["act"]
    HIGHS = 1 + 3 + M1
    assert DENSE % 2 == 0 and len(reader) == DENSE

    def read_by(engine, upto):
        return reader[:upto].count(engine)

    ctx = ExitStack()
    with ctx:
        def sb(name, shape, dt):
            return ctx.enter_context(nc.sbuf_tensor(name, shape, dt))

        def sem(name):
            return ctx.enter_context(nc.semaphore(name))

        KIB = 1024
        arena_at = (nc.sbuf_base + 31) // 32 * 32
        arena = sb("arena", [128, 20 * KIB // 4], fp32)

        weight_arena_at = (nc.sbuf_base + 31) // 32 * 32
        weight_arena = sb("weight_arena", [128, 12 * KIB // 4], fp32)

        def in_arena(name, shape, dt, at):
            return nc.alloc_sbuf_tensor_at(name, shape, dt, offset=arena_at + at)

        def in_weight_arena(name, shape, dt, at):
            return nc.alloc_sbuf_tensor_at(name, shape, dt, offset=weight_arena_at + at)

        raw = in_arena("raw", [128, RAWS, VB * D], fp32, 0)
        w1p_raw = in_weight_arena("w1p_raw", [CHUNK, 3, H1], fp32, 0)
        w1b_raw = in_weight_arena("w1b_raw", [128, H1], fp32, 6 * KIB)
        w2_raw = in_weight_arena("w2_raw", [128, M1, H2], fp32, 8 * KIB)
        pairT = in_weight_arena("pairT", [CHUNK, 2, 3, BLOCK], fp32r, 0)
        gram = in_arena("gram", [GR, PG, JG], fp32, 0)
        h1 = in_arena("h1", [128, 2, M1, BLOCK], fp32r, 0)
        h2 = in_arena("h2", [128, M2, BLOCK], fp32, 16 * KIB)

        embT = sb("embT", [128, HALF, PAD], fp32)
        rows = sb("rows", [128, 2, NG * D], fp32)
        idx = sb("idx", [128, TILES, FEATURES], i32)
        table_at = (nc.sbuf_base + 31) // 32 * 32
        table = sb("table", [128, NO, 2, VB * D], fp32r)
        late_rows = nc.alloc_sbuf_tensor_at("late_rows", [128, 2, NO - 2, D], fp32,
                                            offset=table_at + 2 * 2 * VB * D * 4)
        assert 2 * (NO - 2) * D <= 2 * VB * D
        id_raw = sb("id_raw", [128, 2, 2, HALF], i32)
        hot = sb("hot", [128, 2, 2, VB // 2, HALF], fp32r)
        vocab_i = sb("vocab_i", [128, VB], i32)
        vocab = sb("vocab", [128, VB], fp32)
        ident = sb("ident", [128, 128], fp32)
        packed = sb("packed", [128, GROUP, PAIRS], fp32)
        w1b_more = packed[:, 0:2, 0:H1 // 2]
        bot = sb("bot", [128, GROUP, D], fp32)
        botT = sb("botT", [128, 2, BLOCK], fp32r)
        w1p = sb("w1p", [CHUNK, 2, 3, H1], fp32r)
        w1b = sb("w1b", [128, 2, H1], fp32r)
        w2s = sb("w2s", [128, 2, M1, H2], fp32r)
        w3s = sb("w3s", [128, M2], fp32)
        b1s = sb("b1s", [128, M1], fp32)
        b2s = sb("b2s", [128, M2], fp32)
        y = sb("y", [1, BLOCK], fp32)

        ps_build = [ctx.enter_context(nc.psum_tensor(f"ps_build{i}", [128, 512], fp32)) for i in range(2)]
        ps_gram = [ctx.enter_context(nc.psum_tensor(f"ps_gram{i}", [128, 1024], fp32)) for i in range(2)]
        ps_dense = [ctx.enter_context(nc.psum_tensor(f"ps_dense{i}", [128, 512], fp32)) for i in range(2)]

        consts_made = sem("consts_made")
        weights_in = sem("weights_in")
        idx_in = [sem(f"idx_in{t}") for t in range(TILES)]
        rows_in = [[sem(f"rows_in{s}_{u}") for u in range(TQ)] for s in range(2)]
        late_in = [sem(f"late_in{p}") for p in range(OP)]
        raw_in = [sem(f"raw_in{s}") for s in range(RAWS)]
        id_in = [sem(f"id_in{s}") for s in range(2)]
        bot_in = sem("bot_in")
        pad_set = sem("pad_set")
        table_high = sem("table_high")
        table_low = sem("table_low")
        w1b_added = sem("w1b_added")
        weights_high = sem("weights_high")
        weights_low = sem("weights_low")
        loads_begun = sem("loads_begun")
        gathers_begun = sem("gathers_begun")
        hot_made = sem("hot_made")
        hot_used = sem("hot_used")
        built = sem("built")
        emb_done = sem("emb_done")
        grammed = sem("grammed")
        gram_dve = sem("gram_dve")
        gram_act = sem("gram_act")
        densed = sem("densed")
        relu_done = sem("relu_done")
        high_made = sem("high_made")
        dense_dve = sem("dense_dve")
        dense_act = sem("dense_act")
        dve_step = sem("dve_step")
        out_done = sem("out_done")
        dense_read = {"dve": dense_dve, "act": dense_act}
        WEIGHT_LOADS = 7
        FIRST_STEPS = [(0, (0, 1), 0), (1, (0,), 1), (1, (1,), 2), (2, (0,), 3), (2, (1,), 4), (3, (0, 1), None)]
        def second_steps(i, half):
            more = half == 0 and not half_width(i)
            return [(u, (0, 1), u - 1 if more and u in (1, 2) else None) for u in range(GU)]

        def gram_pieces(t, u, k):
            rows_k = slice(PAD * k, min(PAD * (k + 1), GR))
            src = ps_gram[u % 2][rows_k, :].rearrange("p (h c) -> p h c", h=2)
            src = src[:, :, 0:GB // 2 * GC].rearrange("p h (g c) -> p c h g", g=GB // 2)[:, k * PG:(k + 1) * PG]
            j = (t * GU + u) * GB
            dst = gram[rows_k, :, j:j + GB].rearrange("p f (h g) -> p f h g", h=2)
            return dst, src

        all_banks = ps_dense + [b[:, h * 512:(h + 1) * 512] for b in ps_gram for h in (0, 1)] + ps_build

        def dense_ring(i):
            return all_banks if at_block(i, LAST) else ps_dense

        def dense_at(i, w):
            return dense_ring(i)[w % len(dense_ring(i))]

        def pack_pieces(i, u):
            J = groups(i)
            for n in range(u * RB, min((u + 1) * RB, PG)):
                f = n + 1
                at = f * (f - 1) // 2
                src = dense_at(i, USE_G + u)[0:J, (n % RB) * 128:(n % RB + 1) * 128]
                yield packed[0:J, :, at:at + f], src.rearrange("p (k g) -> p k g", k=GROUP)[:, :, 0:f]

        block = ctx.enter_context(nc.Block())

        @block.sync
        def _(sp):
            def load_idx(at, t):
                sp.dma_start(idx[:, t, :], ids[bass.ds(at + t * TILE, TILE), :]).then_inc(idx_in[t], 16)

            def load_ids(at, n):
                half, p = n // OP, n % OP
                src = ids_onehot[2 * p:2 * p + 2, bass.ds(at + half * HALF, HALF)]
                sp.dma_start(id_raw[:, n % 2, :, :], src.unsqueeze(0).broadcast_to([128, 2, HALF])).then_inc(id_in[n % 2], 16)

            def load_bottom(i, at):
                src = bottom[bass.ds(at, items(i)), :].rearrange("(j k) d -> j k d", k=GROUP)
                sp.dma_start(bot[0:groups(i), :, :], src).then_inc(bot_in, 16)

            def load_table(q):
                src = tables[onehot[q]].rearrange("(p v) d -> p (v d)", v=VB)
                sp.dma_start(raw[0:VP_A, q % RAWS, :], src[0:VP_A, :]).then_inc(raw_in[q % RAWS], 16)
                sp.dma_start(raw[VP_A:VP, q % RAWS, :], src[VP_A:VP, :]).then_inc(raw_in[q % RAWS], 16)

            def store(i, at):
                sp.wait_ge(dense_act, read_by("act", DENSE) * (i + 2))
                sp.sem_inc(loads_begun, 1)
                sp.dma_start(out[bass.ds(at, items(i)), :].rearrange("b o -> o b"), y[:, 0:items(i)]).then_inc(out_done, 16)

            def next_idx(i, at, t):
                for u in range(TQ):
                    sp.wait_ge(rows_in[t % 2][u], 16 * len(bank_slots(u)) * (2 * i + t // 2))
                    sp.sem_inc(loads_begun, 1)
                load_idx(at, t)

            def next_ids(i, at, n):
                sp.wait_ge(hot_made, before(i, HOTS) + 4 * (n - 1))
                sp.sem_inc(loads_begun, 1)
                load_ids(at, n)

            def next_bottom(i, at):
                sp.wait_ge(densed, DENSE * i + USE_R + 1)
                sp.sem_inc(loads_begun, 1)
                load_bottom(i, at)

            load_idx(0, 0)
            load_ids(0, 0)
            load_table(0)
            load_ids(0, 1)
            load_table(1)
            load_table(2)
            load_table(3)
            load_idx(0, 1)
            load_table(4)
            load_idx(HALF, 2)
            load_idx(HALF, 3)
            for q in range(RAWS, NO):
                sp.wait_ge(table_low, q - RAWS + 1)
                load_table(q)
                if q == NO - 2:
                    next_ids(HEAD, 0, 2)
            next_ids(HEAD, 0, 3)
            load_bottom(HEAD, 0)
            for t in range(2):
                for u in range(TQ):
                    sp.wait_ge(rows_in[t][u], 16 * len(bank_slots(u)))
                load_idx(HALF, t)
                next_ids(0, HALF, t)
            next_bottom(0, HALF)
            for n in range(2, OP + 1):
                next_ids(0, HALF, n)
            store(HEAD, 0)
            for n in range(OP + 1, 2 * OP):
                next_ids(0, HALF, n)
            with sp.Fori(1, FULL) as i:
                at = sp.snap(i * BLOCK + HALF)
                at_before = sp.snap(i * BLOCK - HALF)
                next_idx(i, at, 0)
                next_idx(i, at, 1)
                next_idx(i, at, 2)
                next_ids(i, at, 0)
                next_ids(i, at, 1)
                next_idx(i, at, 3)
                next_bottom(i, at)
                for n in range(2, OP + 1):
                    next_ids(i, at, n)
                store(i - 1, at_before)
                for n in range(OP + 1, 2 * OP):
                    next_ids(i, at, n)
            last = BATCH - HALF
            next_idx(LAST, last, 0)
            next_idx(LAST, last, 1)
            next_ids(LAST, last, 0)
            next_bottom(LAST, last)
            store(LAST - 1, last - BLOCK)
            store(LAST, last)
            sp.wait_ge(out_done, 16 * BLOCKS)

        @block.gpsimd
        def _(pool):
            nc.gpsimd.iota(vocab_i[:, :], pattern=[[1, VB]], base=0, channel_multiplier=VB).then_inc(consts_made, 1)
            nc.gpsimd.memset(ident[:, :], 0.0).then_inc(consts_made, 1)
            pool.wait_ge(consts_made, 2)
            nc.gpsimd.affine_select(out=ident[:, :], in_=ident[:, :], compare_op=ALU.not_equal, fill=1.0, base=0,
                                    pattern=[[-1, 128]], channel_multiplier=1).then_inc(consts_made, 1)

            def gather(i, t):
                pool.wait_ge(idx_in[t], 16 * (i + (2 if t < 2 else 1)))
                for u in range(TQ):
                    if t >= 2:
                        pool.wait_ge(built, before(i, BUILDS) + nth(i, "tile", t - 2, u) + 1)
                    elif at_block(i, 0):
                        pool.wait_ge(built, nth(HEAD, "tile", t, u) + 1)
                    elif not at_block(i, HEAD):
                        pool.wait_ge(built, before(i - 1, BUILDS) + nth(i - 1, "tile", t + 2, u) + 1)
                    pool.sem_inc(gathers_begun, 1)
                    for s in bank_slots(u):
                        f = gathered[s]
                        nc.gpsimd.indirect_dma_start(
                            rows[:, t % 2, s * D:(s + 1) * D], None, tables[f],
                            bass.IndirectOffsetOnAxis(idx[:, t, f:f + 1], 0)).then_inc(rows_in[t % 2][u], 16)

            for t in range(2):
                gather(HEAD, t)
            for t in range(TILES):
                gather(0, t)
            with pool.Fori(1, FULL) as i:
                for t in range(TILES):
                    gather(i, t)
            gather(LAST, 0)
            pool.wait_ge(idx_in[1], 16 * (LAST + 2))
            pool.wait_ge(built, before(LAST - 1, BUILDS) + hot_end(LAST - 1, 1, 1))
            for p in LATE_PAIRS:
                for t in range(2):
                    for q in (2 * p, 2 * p + 1):
                        f = onehot[q]
                        nc.gpsimd.indirect_dma_start(
                            late_rows[:, t, q - 2, :], None, tables[f],
                            bass.IndirectOffsetOnAxis(idx[:, t, f:f + 1], 0)).then_inc(late_in[p], 16)
            gather(LAST, 1)

        @block.vector
        def _(dve):
            def low_part(dst, whole, high):
                return nc.vector.tensor_tensor(dst, whole, high.bitcast(fp32), ALU.subtract)

            def split_table(q):
                dve.wait_ge(table_high, q + 1)
                low_part(table[0:VP, q, LOW, :], raw[0:VP, q % RAWS, :], table[0:VP, q, HIGH, :]).then_inc(table_low, 1)

            def make_hot(i, half, p, parts=range(4)):
                n = half * OP + p
                if 0 in parts:
                    dve.wait_ge(id_in[n % 2], 16 * (before(i, OP) + n // 2 + 1))
                for part in parts:
                    q, v0 = part // 2, part % 2
                    if part < 3:
                        if not (at_block(i, HEAD) and n == 0):
                            dve.wait_ge(hot_used, 3 * (before(i, 2 * OP) + n - 1) + part + 1)
                    elif n > 0:
                        dve.wait_ge(built, before(i, BUILDS) + hot_end(i, (n - 1) // OP, (n - 1) % OP))
                    elif at_block(i, 0):
                        dve.wait_ge(built, hot_end(HEAD, 0, OP - 1))
                    elif not at_block(i, HEAD):
                        dve.wait_ge(built, before(i - 1, BUILDS) + hot_end(i - 1, 1, OP - 1))
                    for v in range(VB // 2):
                        row = v0 * VB // 2 + v
                        last = nc.vector.tensor_scalar(hot[0:VP, q, v0, v, :], id_raw[0:VP, n % 2, q, :],
                                                       vocab[0:VP, row:row + 1], None, ALU.is_equal)
                    last.then_inc(hot_made, 1)

            def empty_gram(i, t, u):
                dve.wait_ge(grammed, before(i, GRAMS) + t * GU + u + 1)
                for k in (0, 1):
                    last = nc.vector.tensor_copy(*gram_pieces(t, u, k))
                last.then_inc(gram_dve, 1)

            def pairs_of_half(i, half, next_hot, between=lambda n: None):
                for n in range(2 * GU):
                    empty_gram(i, 2 * half + n // GU, n % GU)
                    between(n)
                    if next_hot and n % 2:
                        make_hot(*next_hot, [n // 2])

            def dense_low(i, w, high_n, dst, high, rows_used=128):
                dve.wait_ge(high_made, HIGHS * (i + 1) + high_n + 1)
                low_part(dst, dense_at(i, w)[0:rows_used, 0:items(i)], high).then_inc(dense_dve, 1)

            def pack(i, u):
                dve.wait_ge(densed, DENSE * (i + 1) + USE_G + u + 1)
                for dst, src in pack_pieces(i, u):
                    last = nc.vector.tensor_copy(dst, src)
                last.then_inc(dense_dve, 1)

            def dense(i, hots):
                for u in range(0, RG, 2):
                    pack(i, u)
                    hots(1, u // 2)
                for c in range(3):
                    dense_low(i, USE_X + c, 1 + c, pairT[:, LOW, c, 0:items(i)], pairT[:, HIGH, c, 0:items(i)], CHUNK)
                hots(2, 0)
                for m in range(M1):
                    if m < 3:
                        hots(2, m + 1)
                    dense_low(i, USE_1 + m, 4 + m, h1[:, LOW, m, 0:items(i)], h1[:, HIGH, m, 0:items(i)])

            def add_w1b():
                dve.wait_ge(weights_in, 16 * WEIGHT_LOADS)
                halves = w1b_raw[:, :].rearrange("p (a b) -> p a b", a=2)
                nc.vector.tensor_tensor(halves, halves, w1b_more, ALU.add).then_inc(w1b_added, 1)

            def split_weights(n):
                if n in (2, 4, 6):
                    dve.wait_ge(weights_high, n // 2)
                if n == 2:
                    low_part(w1p[:, LOW, :, :], w1p_raw[:, :, :], w1p[:, HIGH, :, :]).then_inc(weights_low, 1)
                if n == 4:
                    low_part(w1b[:, LOW, :], w1b_raw[:, :], w1b[:, HIGH, :]).then_inc(weights_low, 1)
                if n == 6:
                    low_part(w2s[:, LOW, :, :], w2_raw[:, :, :], w2s[:, HIGH, :, :]).then_inc(weights_low, 1)

            def bottom_low(i):
                dense_low(i, USE_R, 0, botT[:, LOW, 0:items(i)], botT[:, HIGH, 0:items(i)])

            def first_half(i, next_hot):
                if at_block(i, LAST):
                    dense(i - 1, lambda p, part: None)
                else:
                    dense(i - 1, lambda p, part: make_hot(i, 0, p, [part]))
                    make_hot(i, 0, 3)
                pairs_of_half(i, 0, next_hot)

            def second_half(i):
                for p in range(1, OP):
                    make_hot(i, 1, p)
                bottom_low(i)
                pairs_of_half(i, 1, (i + 1, 0, 0))

            nc.vector.memset(embT[:, :, FEATURES:PAD], 0.0).then_inc(pad_set, 1)
            dve.wait_ge(consts_made, 1)
            nc.vector.tensor_copy(vocab[:, :], vocab_i[:, :]).then_inc(dve_step, 1)
            dve.wait_ge(dve_step, 1)
            for p in range(OP):
                make_hot(HEAD, 0, p, [0])
                split_table(2 * p)
                make_hot(HEAD, 0, p, [1])
                split_table(2 * p + 1)
                make_hot(HEAD, 0, p, [2, 3])
            add_w1b()
            pairs_of_half(HEAD, 0, (0, 0, 0), split_weights)
            bottom_low(HEAD)
            first_half(0, (0, 1, 0))
            second_half(0)
            with dve.Fori(1, FULL) as i:
                first_half(i, (i, 1, 0))
                second_half(i)
            first_half(LAST, None)
            bottom_low(LAST)
            dense(LAST, lambda p, part: None)

        @block.scalar
        def _(act):
            def load_weights():
                for dst, src in ((w1b_raw[:, :], w_bottom_a), (w1b_more, w_bottom_b.rearrange("p (a b) -> p a b", a=2)),
                                 (w1p_raw[:, :, :], w_pairs.rearrange("(c p) h -> p c h", c=3)),
                                 (w2_raw[:, :, :], w2.rearrange("(c p) h -> p c h", p=128)),
                                 (w3s[:, :], w3), (b1s[:, :], b1), (b2s[:, :], b2)):
                    act.dma_start(dst, src).then_inc(weights_in, 16)

            def split_table(q):
                act.wait_ge(raw_in[q % RAWS], 32 * (q // RAWS + 1))
                nc.scalar.copy(table[0:VP, q, HIGH, :], raw[0:VP, q % RAWS, :]).then_inc(table_high, 1)

            def split_weights(n):
                if n == 1:
                    act.wait_ge(weights_in, 16 * WEIGHT_LOADS)
                    nc.scalar.copy(w1p[:, HIGH, :, :], w1p_raw[:, :, :]).then_inc(weights_high, 1)
                if n == 3:
                    act.wait_ge(w1b_added, 1)
                    nc.scalar.copy(w1b[:, HIGH, :], w1b_raw[:, :]).then_inc(weights_high, 1)
                if n == 5:
                    nc.scalar.copy(w2s[:, HIGH, :, :], w2_raw[:, :, :]).then_inc(weights_high, 1)

            def emb_hot(i, half, p):
                s = nth(i, "hot", half, p)
                act.wait_ge(built, before(i, BUILDS) + s + 1)
                nc.scalar.copy(embT[:, :, NG + 2 * p:NG + 2 * p + 2],
                               ps_build[bank_of(i, s)][:, :].rearrange("p (q b) -> p b q", q=2)).then_inc(emb_done, 1)

            def emb_tile(i, t, banks=range(TQ)):
                for u in banks:
                    s = nth(i, "tile", t, u)
                    n = min(FQ, NG - u * FQ)
                    act.wait_ge(built, before(i, BUILDS) + s + 1)
                    src = ps_build[bank_of(i, s)][:, 0:n * 128].rearrange("p (f b) -> p b f", f=n)
                    b = t % 2 * TILE
                    nc.scalar.copy(embT[:, b:b + TILE, u * FQ:u * FQ + n], src).then_inc(emb_done, 1)

            def empty_gram(i, t, u):
                act.wait_ge(grammed, before(i, GRAMS) + t * GU + u + 1)
                for k in (2, 3):
                    last = nc.scalar.copy(*gram_pieces(t, u, k))
                last.then_inc(gram_act, 1)

            def pairs_of_half(i, half, dense=None, between=lambda n: None):
                t = 2 * half
                for u, banks, lookups in FIRST_STEPS:
                    if 1 in banks:
                        empty_gram(i, t, u)
                    if lookups is not None:
                        emb_tile(i, t + 1, [lookups])
                    if u == 0 and dense is not None:
                        layer3(dense)
                    if 1 in banks:
                        between(u)
                for u, banks, lookups in second_steps(i, half):
                    empty_gram(i, t + 1, u)
                    if lookups is not None:
                        emb_tile(i, t + 2, [lookups])
                    between(GU + u)

            def dense_high(i, w, dst, rows_used=128):
                act.wait_ge(densed, DENSE * (i + 1) + w + 1)
                nc.scalar.copy(dst, dense_at(i, w)[0:rows_used, 0:items(i)]).then_inc(high_made, 1)

            def bottom_high(i):
                dense_high(i, USE_R, botT[:, HIGH, 0:items(i)])

            def relayout(i, banks=range(RG)):
                for u in banks:
                    if reader[USE_G + u] == "act":
                        act.wait_ge(densed, DENSE * (i + 1) + USE_G + u + 1)
                        for dst, src in pack_pieces(i, u):
                            last = nc.scalar.copy(dst, src)
                        last.then_inc(dense_act, 1)

            def pair_highs(i, chunks=range(3)):
                for c in chunks:
                    dense_high(i, USE_X + c, pairT[:, HIGH, c, 0:items(i)], CHUNK)

            def layer1(i, between=lambda m: None):
                for m in range(M1):
                    between(m)
                    w = USE_1 + m
                    act.wait_ge(densed, DENSE * (i + 1) + w + 1)
                    bank = dense_at(i, w)[:, 0:items(i)]
                    nc.scalar.activation(bank, bank, ACT.Relu, bias=b1s[:, m:m + 1]).then_inc(relu_done, 1)
                    act.wait_ge(relu_done, M1 * (i + 1) + m + 1)
                    nc.scalar.copy(h1[:, HIGH, m, 0:items(i)], bank).then_inc(high_made, 1)

            def layer2(i, m):
                w = USE_2 + m
                act.wait_ge(densed, DENSE * (i + 1) + w + 1)
                nc.scalar.activation(h2[:, m, 0:items(i)], dense_at(i, w)[:, 0:items(i)], ACT.Relu,
                                     bias=b2s[:, m:m + 1]).then_inc(dense_act, 1)

            def layer3(i):
                act.wait_ge(densed, DENSE * (i + 1) + USE_Y + 1)
                if not at_block(i, HEAD):
                    act.wait_ge(out_done, 16 * (i + 1))
                nc.scalar.copy(y[:, 0:items(i)].rearrange("p (j k) -> p k j", k=GROUP),
                               dense_at(i, USE_Y)[0:1, 0:items(i)].rearrange("p (k j) -> p k j", k=GROUP)).then_inc(dense_act, 1)

            def second_half(i):
                for p in range(OP - 1):
                    emb_tile(i, 2, [p + 2])
                    emb_hot(i, 1, p)
                emb_hot(i, 1, OP - 1)
                bottom_high(i)
                pairs_of_half(i, 1)

            def first_half(i):
                relayout(i - 1)
                emb_hot(i, 0, 0)
                pair_highs(i - 1)
                emb_hot(i, 0, 1)
                layer1(i - 1, lambda m: emb_tile(i, 0, [m]))
                emb_tile(i, 0, [4])
                layer2(i - 1, 0)
                emb_hot(i, 0, 2)
                emb_hot(i, 0, 3)
                layer2(i - 1, 1)
                pairs_of_half(i, 0, i - 1)

            def last_half():
                relayout(LAST - 1, [0])
                emb_tile(LAST, 0, [0])
                relayout(LAST - 1, [1, 2, 3, 4])
                emb_tile(LAST, 0, [1])
                relayout(LAST - 1, [5, 6])
                emb_hot(LAST, 0, 0)
                pair_highs(LAST - 1, [0, 1])
                emb_tile(LAST, 0, [2, 3])
                pair_highs(LAST - 1, [2])
                emb_tile(LAST, 0, [4])
                layer1(LAST - 1, lambda m: emb_hot(LAST, 0, m) if m in (1, 2) else None)
                emb_hot(LAST, 0, 3)
                layer2(LAST - 1, 0)
                layer2(LAST - 1, 1)
                pairs_of_half(LAST, 0, LAST - 1)

            for q in range(NO):
                split_table(q)
                if q == 3:
                    emb_hot(HEAD, 0, 0)
                if q == 5:
                    load_weights()
                    emb_hot(HEAD, 0, 1)
            emb_tile(HEAD, 0)
            emb_hot(HEAD, 0, 2)
            emb_hot(HEAD, 0, 3)
            pairs_of_half(HEAD, 0, None, split_weights)
            bottom_high(HEAD)
            first_half(0)
            second_half(0)
            with act.Fori(1, FULL) as i:
                first_half(i)
                second_half(i)
            last_half()
            bottom_high(LAST)
            relayout(LAST)
            pair_highs(LAST)
            layer1(LAST)
            layer2(LAST, 0)
            layer2(LAST, 1)
            layer3(LAST)

        @block.tensor
        def _(pe):
            def build_bank(i, s):
                def uses(b, upto):
                    return [n for n in range(upto) if bank_of(b, n) == bank_of(i, s)]

                if uses(i, s):
                    pe.wait_ge(emb_done, before(i, BUILDS) + uses(i, s)[-1] + 1)
                elif at_block(i, 0):
                    pe.wait_ge(emb_done, uses(HEAD, BUILDS // 2)[-1] + 1)
                elif not at_block(i, HEAD):
                    pe.wait_ge(emb_done, before(i - 1, BUILDS) + uses(i - 1, BUILDS)[-1] + 1)
                return ps_build[bank_of(i, s)]

            def dense_bank(i, w):
                past = w - len(dense_ring(i))
                if past >= 0:
                    pe.wait_ge(dense_read[reader[past]],
                               read_by(reader[past], DENSE) * (i + 1) + read_by(reader[past], past + 1))
                return dense_at(i, w)

            def onehot_pair(i, half, p, parts=range(4)):
                n = half * OP + p
                s = nth(i, "hot", half, p)
                bank = build_bank(i, s) if 0 in parts else ps_build[bank_of(i, s)]
                for part in parts:
                    q, v0 = part // 2, part % 2
                    if at_block(i, HEAD) and v0 == 0:
                        pe.wait_ge(table_low, 2 * p + q + 1)
                    pe.wait_ge(hot_made, before(i, HOTS) + 4 * n + part + 1)
                    for v in range(VB // 2):
                        row = (v0 * VB // 2 + v) * D
                        for bits in (HIGH, LOW):
                            last = nc.tensor.matmul(bank[:, q * HALF:(q + 1) * HALF],
                                                    table[0:VP, 2 * p + q, bits, row:row + D],
                                                    hot[0:VP, q, v0, v, :], start=(v0 == v == bits == 0),
                                                    stop=(v0 == 1 and v == VB // 2 - 1 and bits == LOW))
                    last.then_inc(hot_used if part < 3 else built, 1)

            def transpose_tile(i, t, banks=range(TQ)):
                for u in banks:
                    pe.wait_ge(rows_in[t % 2][u], 16 * len(bank_slots(u)) * (before(i, 2) + t // 2 + 1))
                    bank = build_bank(i, nth(i, "tile", t, u))
                    for f, s in enumerate(bank_slots(u)):
                        last = nc.tensor.transpose(bank[:, f * 128:(f + 1) * 128], rows[:, t % 2, s * D:(s + 1) * D],
                                                   ident[:, :])
                    last.then_inc(built, 1)

            def transpose_late(p):
                pe.wait_ge(late_in[p], 16 * 4)
                bank = build_bank(LAST, nth(LAST, "hot", 0, p))
                for q in range(2):
                    for t in range(2):
                        c = q * HALF + t * TILE
                        last = nc.tensor.transpose(bank[:, c:c + TILE], late_rows[:, t, 2 * p + q - 2, :], ident[:, :])
                last.then_inc(built, 1)

            def pair_products(i, t, u, banks):
                v = t * GU + u
                if 0 in banks:
                    if u == 0:
                        pe.wait_ge(emb_done, before(i, BUILDS) + max(tile_end(i, t), hot_end(i, t // 2, OP - 1)))
                    if v >= 2:
                        pe.wait_ge(gram_dve, before(i, GRAMS) + v - 1)
                        pe.wait_ge(gram_act, before(i, GRAMS) + v - 1)
                for b in banks:
                    for g in range(GB // 2):
                        at = t % 2 * TILE + (u * GB + b * GB // 2 + g) * GROUP
                        c = b * 512 + g * GC
                        last = nc.tensor.matmul(ps_gram[u % 2][0:GR, c:c + GC],
                                                embT[:, at:at + GROUP, :].rearrange("p k g -> p (k g)")[:, 0:GR],
                                                embT[:, at:at + GROUP, 1:FEATURES], start=True, stop=True)
                if 1 in banks:
                    last.then_inc(grammed, 1)

            def bottom_back(i):
                pe.wait_ge(bot_in, 16 * (i + 2))
                if not at_block(i, HEAD):
                    pe.wait_ge(dense_act, read_by("act", DENSE) * (i + 1))
                J = groups(i)
                for k in range(GROUP):
                    last = nc.tensor.transpose(dense_at(i, USE_R)[:, k * J:(k + 1) * J], bot[0:J, k, :], ident[0:J, 0:J])
                last.then_inc(densed, 1)

            def relayout(i, banks):
                J = groups(i)
                if 0 in banks:
                    pe.wait_ge(gram_dve, before(i, GRAMS) + J // GB)
                    pe.wait_ge(gram_act, before(i, GRAMS) + J // GB)
                for u in banks:
                    bank = dense_bank(i, USE_G + u)
                    for n in range(u * RB, min((u + 1) * RB, PG)):
                        last = nc.tensor.transpose(bank[0:J, (n % RB) * 128:(n % RB) * 128 + GR], gram[0:GR, n, 0:J],
                                                   ident[0:GR, 0:GR])
                    last.then_inc(densed, 1)

            def wait_dense(i, upto):
                for e in ("dve", "act"):
                    pe.wait_ge(dense_read[e], read_by(e, DENSE) * (i + 1) + read_by(e, upto))

            def pairs_back(i, chunks):
                J = groups(i)
                if 0 in chunks:
                    wait_dense(i, USE_X)
                for c in chunks:
                    bank = dense_bank(i, USE_X + c)
                    for k in range(GROUP):
                        last = nc.tensor.transpose(bank[0:CHUNK, k * J:(k + 1) * J],
                                                   packed[0:J, k, c * CHUNK:(c + 1) * CHUNK], ident[0:J, 0:J])
                    last.then_inc(densed, 1)

            def split_product(bank, w, x, first=False, end=False):
                for m, (a, b) in enumerate(((HIGH, HIGH), (HIGH, LOW), (LOW, HIGH))):
                    last = nc.tensor.matmul(bank, w(a), x(b), start=(first and m == 0), stop=(end and m == 2))
                return last

            def layer1(i, between=lambda m: None):
                def bottom_part(m):
                    if m == 0:
                        wait_dense(i, USE_G)
                    if m == 0 and at_block(i, HEAD):
                        pe.wait_ge(weights_low, 3)
                    split_product(dense_bank(i, USE_1 + m)[:, 0:items(i)], lambda a: w1b[:, a, m * 128:(m + 1) * 128],
                                  lambda b: botT[:, b, 0:items(i)], first=True)

                if at_block(i, LAST):
                    for m in range(M1):
                        bottom_part(m)
                for m in range(M1):
                    between(m)
                    if not at_block(i, LAST):
                        bottom_part(m)
                    if m == 0:
                        wait_dense(i, USE_1)
                    for c in range(3):
                        last = split_product(dense_at(i, USE_1 + m)[:, 0:items(i)],
                                             lambda a: w1p[:, a, c, m * 128:(m + 1) * 128],
                                             lambda b: pairT[:, b, c, 0:items(i)], end=(c == 2))
                    last.then_inc(densed, 1)

            def layer2(i, m, chunks=range(M1)):
                w = USE_2 + m
                bank = dense_bank(i, w) if 0 in chunks else dense_at(i, w)
                cols = slice(m * 128, (m + 1) * 128)
                for c in chunks:
                    if m == 0:
                        wait_dense(i, USE_1 + c + 1)
                    last = split_product(bank[:, 0:items(i)], lambda a: w2s[:, a, c, cols], lambda b: h1[:, b, c, 0:items(i)],
                                         first=(c == 0), end=(c == M1 - 1))
                if M1 - 1 in chunks:
                    last.then_inc(densed, 1)

            def layer3(i):
                bank = dense_bank(i, USE_Y)
                for c in range(M2):
                    wait_dense(i, USE_2 + c + 1)
                    last = nc.tensor.matmul(bank[0:1, 0:items(i)], w3s[:, c:c + 1], h2[:, c, 0:items(i)],
                                            start=(c == 0), stop=(c == M2 - 1))
                last.then_inc(densed, 1)

            def pairs_of_half(i, half, dense=None):
                t = 2 * half
                for u, banks, lookups in FIRST_STEPS:
                    pair_products(i, t, u, banks)
                    if lookups is not None:
                        transpose_tile(i, t + 1, [lookups])
                    if u == 0 and dense is not None:
                        layer3(dense)
                for u, banks, lookups in second_steps(i, half):
                    pair_products(i, t + 1, u, banks)
                    if lookups is not None:
                        transpose_tile(i, t + 2, [lookups])

            def second_half(i):
                for p in range(OP - 1):
                    onehot_pair(i, 1, p, [0, 1])
                    transpose_tile(i, 2, [p + 2])
                    onehot_pair(i, 1, p, [2, 3])
                onehot_pair(i, 1, OP - 1)
                bottom_back(i)
                pairs_of_half(i, 1)

            def first_half(i):
                onehot_pair(i, 0, 0, [0])
                relayout(i - 1, [0])
                onehot_pair(i, 0, 0, [1])
                relayout(i - 1, [1, 2])
                onehot_pair(i, 0, 0, [2])
                relayout(i - 1, [3, 4])
                onehot_pair(i, 0, 0, [3])
                relayout(i - 1, [5, 6])
                onehot_pair(i, 0, 1, [0])
                pairs_back(i - 1, [0, 1])
                onehot_pair(i, 0, 1, [1])
                pairs_back(i - 1, [2])
                onehot_pair(i, 0, 1, [2, 3])
                layer1(i - 1, lambda m: transpose_tile(i, 0, [m]))
                layer2(i - 1, 0, [0, 1, 2])
                transpose_tile(i, 0, [4])
                layer2(i - 1, 0, [3])
                onehot_pair(i, 0, 2)
                onehot_pair(i, 0, 3)
                layer2(i - 1, 1)
                pairs_of_half(i, 0, i - 1)

            def last_half():
                onehot_pair(LAST, 0, 0, [0])
                relayout(LAST - 1, [0])
                transpose_tile(LAST, 0, [0])
                relayout(LAST - 1, [1, 2])
                onehot_pair(LAST, 0, 0, [1])
                relayout(LAST - 1, [3, 4])
                onehot_pair(LAST, 0, 0, [2])
                transpose_tile(LAST, 0, [1])
                relayout(LAST - 1, [5, 6])
                onehot_pair(LAST, 0, 0, [3])
                pairs_back(LAST - 1, [0, 1])
                transpose_tile(LAST, 0, [2, 3])
                pairs_back(LAST - 1, [2])
                transpose_tile(LAST, 0, [4])
                layer1(LAST - 1, lambda m: transpose_late(m) if m in (1, 2) else None)
                layer2(LAST - 1, 0, [0, 1, 2])
                transpose_late(3)
                layer2(LAST - 1, 0, [3])
                layer2(LAST - 1, 1)
                pairs_of_half(LAST, 0, LAST - 1)

            pe.wait_ge(consts_made, 3)
            onehot_pair(HEAD, 0, 0)
            onehot_pair(HEAD, 0, 1)
            transpose_tile(HEAD, 0)
            onehot_pair(HEAD, 0, 2)
            onehot_pair(HEAD, 0, 3)
            pe.wait_ge(pad_set, 1)
            pairs_of_half(HEAD, 0)
            bottom_back(HEAD)
            first_half(0)
            second_half(0)
            with pe.Fori(1, FULL) as i:
                first_half(i)
                second_half(i)
            last_half()
            bottom_back(LAST)
            relayout(LAST, range(RG))
            pairs_back(LAST, range(3))
            layer1(LAST)
            for chunks in (range(M1 - 1), [M1 - 1]):
                for m in range(M2):
                    layer2(LAST, m, chunks)
            layer3(LAST)


def kernel(**inputs):
    import numpy as _np
    import concourse.bacc as _bacc
    from concourse import mybir as _mybir
    from concourse.bass_utils import run_bass_kernel_spmd as _run

    nc = _bacc.Bacc("TRN2", target_bir_lowering=False, num_devices=1)
    tables = [_np.asarray(inputs[f"tbl_{f}"]) for f in range(FEATURES)]
    ids = _np.asarray(inputs["ids"])
    w1 = _np.asarray(inputs["W_top1"])
    gathered, onehot = slots([t.shape[0] for t in tables])
    layouts = {
        "bottom": _np.asarray(inputs["r_bottom_mlp_out"]),
        "ids": ids,
        "ids_onehot": ids[:, onehot].T,
        "w_bottom_a": w1[0:D],
        "w_pairs": w1[pair_rows(gathered + onehot)],
        "w_bottom_b": w1[D + PAIRS:],
        "b1": _np.asarray(inputs["b_top1"]).reshape(H1 // 128, 128).T,
        "w2": _np.asarray(inputs["W_top2"]),
        "b2": _np.asarray(inputs["b_top2"]).reshape(H2 // 128, 128).T,
        "w3": _np.asarray(inputs["W_top3"]).reshape(H2 // 128, 128).T,
    }
    arrays, args = {}, {}

    def operand(name, a):
        a = _np.ascontiguousarray(a)
        arrays[name + "_dram"] = a
        return nc.dram_tensor(name + "_dram", a.shape, _mybir.dt.from_np(a.dtype), kind="ExternalInput").ap()

    for name, a in layouts.items():
        args[name] = operand(name, a)
    args["tables"] = [operand(f"tbl_{f}", t) for f, t in enumerate(tables)]
    args["out"] = nc.dram_tensor("y_dram", (BATCH, 1), _mybir.dt.float32, kind="ExternalOutput").ap()
    dlrm_tower(nc, **args)
    r = _run(nc, [arrays], core_ids=[0])
    return r.results[0]["y_dram"]
```
